# Optimizing a Trainium2 kernel written in Bass

```python
import numpy as np
import jax
import jax.numpy as jnp

def _softmax(x, axis=-1):
    return jax.nn.softmax(x, axis=axis)

def _gelu(x):
    return jax.nn.gelu(x, approximate=True)

def _silu(x):
    return jax.nn.silu(x)

def _sigmoid(x):
    return jax.nn.sigmoid(x)

def _layernorm(x, axis=-1, eps=1e-05):
    m = jnp.mean(x, axis=axis, keepdims=True)
    v = jnp.var(x, axis=axis, keepdims=True)
    return (x - m) / jnp.sqrt(v + eps)

def _scatter_add(tgt, idx, src, axis=0):
    return tgt.at[idx].add(src)

def _segment_sum(src, seg, n):
    return jax.ops.segment_sum(src, seg, n)
kernel_name = 'mk_adj_ffn_d1_adj_r2_de0453'

def setup_inputs(seed: int=0):
    np.random.seed(seed)
    _w = jnp.asarray

    def _rec_inputs():
        import jax
        import jax.numpy as jnp
        _gk = jax.random.key(seed)
        x = -0.000929 + 1 * jax.random.normal(jax.random.fold_in(_gk, 1), (128, 64, 256), jnp.float32)
        _a = jax.random.bernoulli(jax.random.fold_in(_gk, 2), 0.0625, (64, 64))
        adj = _a.astype(jnp.int32)
        return (x, adj)
    x, adj = _rec_inputs()

    def _L0_gnn_setup():
        import jax, jax.numpy as jnp
        import numpy as np
        B, K, DIN, DOUT = (32, 64, 256, 256)
        key = jax.random.key(seed)
        k1, k2, k3, k4 = jax.random.split(key, 4)
        x = jax.random.normal(k1, (B, K, DIN), dtype=jnp.float32)
        adj = jax.random.randint(k2, (K, K), 0, 2, dtype=jnp.int32)
        W = jax.random.normal(k3, (DOUT, 2 * DIN), dtype=jnp.float32) * 0.02
        b = jax.random.normal(k4, (DOUT,), dtype=jnp.float32) * 0.02
        return {'x': x, 'adj': adj, 'W': W, 'b': b}
    _L0_gnn_all = _L0_gnn_setup()
    _L0_gnn_in = {k: v for k, v in _L0_gnn_all.items() if k in ('W', 'b')}
    del _L0_gnn_all

    def _L0_ffn_setup():
        import jax, jax.numpy as jnp
        import numpy as np
        NUM_EXPERTS = 8
        TOP_K = 2
        key = jax.random.key(seed)
        ks = jax.random.split(key, 5)
        B, N, E, H, X = (8, 1024, 256, 384, NUM_EXPERTS)
        s_in = 0.02
        return {'x': jax.random.normal(ks[0], (B, N, E), dtype=jnp.float32), 'Wg': jax.random.normal(ks[1], (E, X), dtype=jnp.float32) * s_in, 'bg': jnp.zeros((X,), dtype=jnp.float32), 'W1': jax.random.normal(ks[2], (X, E, H), dtype=jnp.float32) * (1.0 / np.sqrt(E)), 'b1': jnp.zeros((X, H), dtype=jnp.float32), 'W2': jax.random.normal(ks[3], (X, H, E), dtype=jnp.float32) * (1.0 / np.sqrt(H)), 'b2': jnp.zeros((X, E), dtype=jnp.float32)}
    _L0_ffn_all = _L0_ffn_setup()
    _L0_ffn_in = {k: v for k, v in _L0_ffn_all.items() if k in ('Wg', 'bg', 'W1', 'b1', 'W2', 'b2')}
    del _L0_ffn_all
    return {'x': x, 'adj': adj, 'L0_gnn_W': _L0_gnn_in['W'], 'L0_gnn_b': _L0_gnn_in['b'], 'L0_ffn_Wg': _L0_ffn_in['Wg'], 'L0_ffn_bg': _L0_ffn_in['bg'], 'L0_ffn_W1': _L0_ffn_in['W1'], 'L0_ffn_b1': _L0_ffn_in['b1'], 'L0_ffn_W2': _L0_ffn_in['W2'], 'L0_ffn_b2': _L0_ffn_in['b2']}

def reference(x, adj, L0_gnn_W, L0_gnn_b, L0_ffn_Wg, L0_ffn_bg, L0_ffn_W1, L0_ffn_b1, L0_ffn_W2, L0_ffn_b2):
    import jax
    import jax.numpy as jnp

    def _L0_gnn_ref(x, adj, W, b):
        import jax, jax.numpy as jnp
        import numpy as np
        B, K, DIN, DOUT = (32, 64, 256, 256)
        Din = x.shape[-1]
        Wi, Wj = (W[:, :Din], W[:, Din:])
        mi = jnp.einsum('bkd,od->bko', x, Wi)
        mj = jnp.einsum('bkd,od->bko', x, Wj)
        a = adj.astype(x.dtype)
        deg = a.sum(axis=1)
        out = deg[None, :, None] * (mi + b) + jnp.einsum('ij,bjo->bio', a, mj)
        return out

    def _L0_ffn_ref(x, Wg, bg, W1, b1, W2, b2):
        import jax, jax.numpy as jnp
        import numpy as np
        NUM_EXPERTS = 8
        TOP_K = 2
        scores = jnp.einsum('bne,ex->bnx', x, Wg) + bg
        topk_vals, topk_idx = jax.lax.top_k(scores, TOP_K)
        gates = jax.nn.softmax(topk_vals, axis=-1)
        h = jnp.einsum('bne,xeh->bnxh', x, W1) + b1
        h = jax.nn.gelu(h, approximate=False)
        expert_out = jnp.einsum('bnxh,xhe->bnxe', h, W2) + b2
        onehot = jax.nn.one_hot(topk_idx, NUM_EXPERTS, dtype=x.dtype)
        combine = jnp.einsum('bnk,bnkx->bnx', gates, onehot)
        out = jnp.einsum('bnx,bnxe->bne', combine, expert_out)
        return out
    x = x + _L0_gnn_ref(_layernorm(x, axis=-1), adj, L0_gnn_W, L0_gnn_b)
    x = x + _L0_ffn_ref(_layernorm(x, axis=-1), L0_ffn_Wg, L0_ffn_bg, L0_ffn_W1, L0_ffn_b1, L0_ffn_W2, L0_ffn_b2)
    return x

_drawn_inputs = setup_inputs


def setup_inputs(seed=0):
    import zlib

    import numpy as np

    out = dict(_drawn_inputs(seed))
    spreads = {'L0_ffn_bg': (0.0, 0.1), 'L0_ffn_b1': (0.0, 0.324), 'L0_ffn_b2': (0.0, 0.1)}
    factors = {}
    for name, (base, spread) in spreads.items():
        noise = np.random.default_rng([zlib.crc32(name.encode()), seed]).standard_normal(out[name].shape)
        drawn = base * np.exp(spread * noise) if base else spread * noise
        out[name] = jnp.asarray(drawn.astype(out[name].dtype))
    for name, factor in factors.items():
        out[name] = (out[name] * factor).astype(out[name].dtype)
    return out
```

```python
def build(nc, x, adj, adj_t, gnn_wt, gnn_b, wg, bg, w1, b1_t, w2, b2, consts_f, consts_h, out):
    from contextlib import ExitStack

    import concourse.bass as bass
    from concourse import mybir

    F32, F16, BF16 = mybir.dt.float32, mybir.dt.float16, mybir.dt.bfloat16
    I32, U32 = mybir.dt.int32, mybir.dt.uint32
    ALU = mybir.AluOpType
    ACT = mybir.ActivationFunctionType
    AX_X = mybir.AxisListType.X
    ds = bass.ds

    P = 128
    B, NODES, D = x.shape
    TOKENS = B * NODES
    TILES = TOKENS // P
    EXPERTS, _, H = w1.shape
    GROUP = 4
    GROUPS = TILES // GROUP
    DC, HC = D // P, H // P
    EPS = 1e-5
    X_SCALE = 256.0
    W_SCALE = 1024.0
    H_SCALE = 64.0
    BLOCK = 256
    HALVES = BLOCK // P
    LIST_ROWS = TOKENS + BLOCK
    BLOCKS = 2 * TOKENS // BLOCK + EXPERTS
    ZERO_LIST = EXPERTS * LIST_ROWS
    ROWS = ZERO_LIST + BLOCK
    ROW32 = D + EXPERTS
    ROW16 = 2 * ROW32
    NOWHERE = 1 << 20
    RING = 4 * GROUP
    WCOLS = DC * H
    WRING = 4

    col = 0
    cols = {}
    for name, n in (("ident", P), ("iota", 2 * GROUP * EXPERTS), ("list_start", GROUP * EXPERTS),
                    ("token", TILES), ("mask", 3), ("mask3", 1), ("block_row", BLOCKS), ("block", BLOCKS),
                    ("whole", EXPERTS * (TOKENS // BLOCK)), ("zero", EXPERTS), ("eps", 1)):
        cols[name] = (col, n)
        col += n
    NCF = col

    lists = nc.dram_tensor("lists", [ROWS, ROW32], I32).ap()
    lists16 = lists.bitcast(F16)
    parts = nc.dram_tensor("parts", [2 * TOKENS, D], F32).ap()

    with ExitStack() as ctx:
        def sb(name, shape, dt):
            return ctx.enter_context(nc.sbuf_tensor(name, shape, dt))

        def sem(name):
            return ctx.enter_context(nc.semaphore(name))

        bank = [ctx.enter_context(nc.psum_tensor(f"bank{i}", [P, 512], F32)) for i in range(8)]
        ps_nb = bank[0:2]
        ps_gnn = bank[2:4]
        ps_score = bank[4]
        ps_place = bank[5]
        ps_h = [bank[0:3], bank[3:6]]
        ps_y = bank[6:8]

        X = sb("X", [P, TILES * D], F32)
        cf = sb("cf", [P, NCF], F32)
        ch = sb("ch", [P, 2 * P], F16)

        def const(name):
            a, n = cols[name]
            return cf[:, a:a + n]

        below, ones = ch[:, 0:P], ch[:, P:2 * P]

        adj_i = sb("adj_i", [P, NODES], I32)
        adj_f = sb("adj_f", [P, NODES], F32)
        adjt_i = sb("adjt_i", [P, P], I32)
        deg = sb("deg", [P, 1], F32)
        nb = sb("nb", [P, 2 * P], F16)
        deg_rows = sb("deg_rows", [P, P], F16)
        gw = sb("gw", [P, 2 * DC * D], F32)
        bias_rows = sb("bias_rows", [P, D], BF16)
        bb = sb("bb", [P, D], F32)
        bpart = sb("bpart", [P, 3 * D], BF16)
        brest = sb("brest", [P, 2 * D], F32)
        bmask = sb("bmask", [P, 2 * D], F32)
        wg_f = sb("wg_f", [P, DC * EXPERTS], F32)
        wg_s = sb("wg_s", [P, DC * EXPERTS], F32)
        wg_h = sb("wg_h", [P, 2 * DC * EXPERTS], F16)
        bg4 = sb("bg4", [P, GROUP * EXPERTS], F32)

        stat1 = sb("stat1", [P, 2 * 6], F32)
        stat2 = sb("stat2", [P, 2 * 6], F32)
        mv1 = sb("mv1", [P, GROUP * 2], F32)
        mv2 = sb("mv2", [P, GROUP * 2], F32)
        sd1 = sb("sd1", [P, GROUP], F32)
        sd2 = sb("sd2", [P, GROUP], F32)
        rs1 = sb("rs1", [P, TILES], F32)
        nm1 = sb("nm1", [P, TILES], F32)
        rs2 = sb("rs2", [P, TILES], F32)
        nm2 = sb("nm2", [P, TILES], F32)
        xf1 = sb("xf1", [P, 2 * D], F32)
        xn1 = sb("xn1", [P, 2 * 2 * D], F16)
        z = sb("z", [P, 2 * 2 * D], F32)
        xf2 = sb("xf2", [P, 2 * D], F32)
        row = sb("row", [P, RING * ROW32], I32)
        row16 = row[:, :].bitcast(F16)
        gT = sb("gT", [P, GROUP * 2 * DC * P], F16)
        score = sb("score", [P, GROUP * EXPERTS], F32)
        best = sb("best", [P, GROUP * 8], F32)
        best_i = sb("best_i", [P, GROUP * 8], U32)
        best_f = sb("best_f", [P, GROUP * 2], F32)
        chose2 = sb("chose2", [P, GROUP * 2 * EXPERTS], F32)
        chose = sb("chose", [P, GROUP * EXPERTS], F16)
        chose_g = sb("chose_g", [P, EXPERTS], F32)
        before = sb("before", [P, EXPERTS], F16)
        place_e = sb("place_e", [P, GROUP * EXPERTS], F32)
        place2 = sb("place2", [P, GROUP * 2 * EXPERTS], F32)
        place_f = sb("place_f", [P, GROUP * 2], F32)
        place = sb("place", [P, RING * 2], I32)
        gap = sb("gap", [P, TILES], F32)

        w_in = sb("w_in", [P, WRING * WCOLS], F32)
        w_sc = sb("w_sc", [P, WCOLS], F32)
        cuts = sb("cuts", [P, 4 * EXPERTS * WCOLS], F16)
        w1h, w1l, w2h, w2l = (cuts[:, i * EXPERTS * WCOLS:(i + 1) * EXPERTS * WCOLS] for i in range(4))
        b1s = sb("b1s", [P, EXPERTS * HC], F32)
        b2s = sb("b2s", [P, EXPERTS * D], F32)

        count = sb("count", [P, EXPERTS], F32)
        full = sb("full", [P, EXPERTS * (TOKENS // BLOCK)], F32)
        nblk = sb("nblk", [P, EXPERTS], F32)
        cum = sb("cum", [P, EXPERTS], F32)
        skip = sb("skip", [P, EXPERTS], F32)
        passed = sb("passed", [P, BLOCKS * EXPERTS], F32)
        skipped = sb("skipped", [P, BLOCKS * EXPERTS], F32)
        owner_f = sb("owner_f", [P, BLOCKS], F32)
        start_f = sb("start_f", [P, 2 * BLOCKS], F32)
        owner = sb("owner", [P, BLOCKS], I32)
        weights_at = sb("weights_at", [P, BLOCKS], I32)
        start = sb("start", [P, BLOCKS], I32)
        list_end = sb("list_end", [P, EXPERTS], I32)
        zeros = sb("zeros", [P, HALVES * ROW32], I32)

        xT = sb("xT", [P, 2 * 2 * DC * BLOCK], F16)
        dest = sb("dest", [P, 2 * HALVES], I32)
        HCOLS = 2 * HC * BLOCK
        hf = w_in[:, 0:HCOLS]
        hh = w_in[:, HCOLS:HCOLS + HCOLS // 2].bitcast(F16)
        hl = w_in[:, HCOLS + HCOLS // 2:2 * HCOLS].bitcast(F16)
        y = sb("y", [P, 2 * HALVES * D], F32)

        CR = 4
        pt = cuts[:, 0:2 * CR * 2 * GROUP * D].bitcast(F32)
        ge = sb("ge", [P, TILES], F32)
        gd = sb("gd", [P, TILES], F32)
        g0 = sb("g0", [P, TILES], F32)
        g1 = sb("g1", [P, TILES], F32)

        s_const = sem("s_const")
        s_adjz = sem("s_adjz")
        s_adj = sem("s_adj")
        s_setup = sem("s_setup")
        s_nb = sem("s_nb")
        s_degp = sem("s_degp")
        s_deg = sem("s_deg")
        s_bias = sem("s_bias")
        s_wgr = sem("s_wgr")
        s_x = sem("s_x")
        s_bn1 = sem("s_bn1")
        s_mv1 = sem("s_mv1")
        s_sd1 = sem("s_sd1")
        s_rs1 = sem("s_rs1")
        s_nm1 = sem("s_nm1")
        s_bn2 = sem("s_bn2")
        s_mv2 = sem("s_mv2")
        s_sd2 = sem("s_sd2")
        s_rs2 = sem("s_rs2")
        s_nm2 = sem("s_nm2")
        s_hi1 = sem("s_hi1")
        s_lo1 = sem("s_lo1")
        s_nbp = sem("s_nbp")
        s_z = sem("s_z")
        s_gnn = sem("s_gnn")
        s_x1 = sem("s_x1")
        s_hi2 = sem("s_hi2")
        s_lo2 = sem("s_lo2")
        s_gT = [sem(f"s_gT{j}") for j in range(GROUP)]
        s_sp = sem("s_sp")
        s_score = sem("s_score")
        s_route = sem("s_route")
        s_chose = sem("s_chose")
        s_pp = sem("s_pp")
        s_step = sem("s_step")
        s_place = sem("s_place")
        s_scat = [sem(f"s_scat{j}") for j in range(RING // GROUP)]
        s_free = sem("s_free")
        s_w = [sem(f"s_w{k}") for k in range(WRING)]
        s_wsc = sem("s_wsc")
        s_wh = sem("s_wh")
        s_wl = sem("s_wl")
        s_zeros = sem("s_zeros")
        s_cntp = sem("s_cntp")
        s_tab = sem("s_tab")
        s_tables = sem("s_tables")
        s_pad = sem("s_pad")
        s_listed = sem("s_listed")
        s_xT = [sem(f"s_xT{k}") for k in range(2)]
        s_dest = [sem(f"s_dest{k}") for k in range(2)]
        s_hp = sem("s_hp")
        s_gelu = sem("s_gelu")
        s_hh = sem("s_hh")
        s_hl = sem("s_hl")
        s_yp = sem("s_yp")
        s_y = sem("s_y")
        s_part = [sem(f"s_part{k}") for k in range(2)]
        s_ge = sem("s_ge")
        s_gate = sem("s_gate")
        s_pt = [sem(f"s_pt{k}") for k in range(CR)]
        s_sum0 = sem("s_sum0")
        s_sum = sem("s_sum")
        s_out = sem("s_out")
        s_apart = sem("s_apart")

        x_dram = x.rearrange("b k d -> (b k) d").rearrange("(t p) d -> p t d", p=P)
        out_dram = out.rearrange("b k d -> (b k) d").rearrange("(t p) d -> p t d", p=P)
        X3 = X[:, :].rearrange("p (t d) -> p t d", d=D)

        N_CONST = 11

        def in_loop(s):
            return not isinstance(s, int)

        def has(s, g):
            return in_loop(s) or 0 <= g < GROUPS

        def has_tile(s, t):
            return in_loop(s) or 0 <= t < TILES

        def wait(eng, semaphore, value):
            if not isinstance(value, int) or value > 0:
                eng.wait_ge(semaphore, value)

        def apart(eng, s):
            if in_loop(s):
                eng.sem_inc(s_apart, 1)

        def ring(g):
            return (g % (RING // GROUP)) * GROUP

        block = ctx.enter_context(nc.Block())

        @block.sync
        def _(sp):
            sp.dma_start(X3[:, 0:GROUP, :], x_dram[:, 0:GROUP, :]).then_inc(s_x, 16)
            sp.wait_ge(s_adjz, 1)
            sp.dma_start(adjt_i[0:NODES, 0:NODES], adj_t).then_inc(s_adj, 16)
            sp.dma_start(adjt_i[NODES:P, NODES:P], adj_t).then_inc(s_adj, 16)
            sp.dma_start(adj_i[0:NODES, :], adj).then_inc(s_adj, 16)
            sp.dma_start(adj_i[NODES:P, :], adj).then_inc(s_adj, 16)
            for g in range(1, 4):
                sp.wait_ge(s_x, 16 * g)
                sp.dma_start(X3[:, g * GROUP:(g + 1) * GROUP, :],
                             x_dram[:, g * GROUP:(g + 1) * GROUP, :]).then_inc(s_x, 16)

            def transposes(g):
                for j in range(GROUP):
                    t = g * GROUP + j
                    sp.wait_ge(s_lo2, t + 1)
                    apart(sp, g)
                    wait(sp, s_sp, t - GROUP + 1)
                    apart(sp, g)
                    sp.dma_start_transpose(
                        gT[:, j * 2 * D:(j + 1) * 2 * D].rearrange("p (c t) -> p c t", t=P),
                        row16[:, ds((ring(g) + j) * ROW16, 2 * D)]).then_inc(s_gT[j], 16)

            def load_and_transpose(g):
                sp.wait_ge(s_x, (g + 4) * 16)
                sp.dma_start(X3[:, ds((g + 4) * GROUP, GROUP), :],
                             x_dram[:, ds((g + 4) * GROUP, GROUP), :]).then_inc(s_x, 16)
                transposes(g)

            load_and_transpose(0)
            with sp.Fori(1, GROUPS - 4) as g:
                load_and_transpose(g)
            with sp.Fori(GROUPS - 4, GROUPS) as g:
                transposes(g)

            sp.wait_ge(s_zeros, 1)
            sp.wait_ge(s_tables, 1)
            for e in range(EXPERTS):
                r = sp.value_load(list_end[0:1, e:e + 1], min_val=0, max_val=ROWS - BLOCK)
                sp.dma_start(lists[ds(r, BLOCK), :].rearrange("(p h) c -> p (h c)", h=HALVES),
                             zeros[:, :]).then_inc(s_pad, 16)
            sp.dma_start(lists[ZERO_LIST:ROWS, :].rearrange("(p h) c -> p (h c)", h=HALVES),
                         zeros[:, :]).then_inc(s_pad, 16)
            sp.wait_ge(s_pad, 16 * (EXPERTS + 1))
            sp.wait_ge(s_listed, 1)
            sp.wait_ge(s_tables, 2)

            def load_rows(b, k):
                r = sp.value_load(start[0:1, ds(b, 1)], min_val=0, max_val=ROWS - BLOCK)
                wait(sp, s_hp, HC * (b - 1))
                sp.dma_start_transpose(
                    xT[:, k * 2 * DC * BLOCK:(k + 1) * 2 * DC * BLOCK]
                    .rearrange("p (c t) -> p c t", t=BLOCK),
                    lists16[ds(r, BLOCK), 0:2 * D]).then_inc(s_xT[k], 16)

            def load_dest(b, k, n):
                r = sp.value_load(start[0:1, ds(b, 1)], min_val=0, max_val=ROWS - BLOCK)
                e = sp.value_load(owner[0:1, ds(b, 1)], min_val=0, max_val=EXPERTS - 1)
                wait(sp, s_part[k], 16 * HALVES * n)
                sp.dma_start(dest[:, k * HALVES:(k + 1) * HALVES],
                             lists[ds(r, BLOCK), ds(e + D, 1)].rearrange("(h p) c -> p (h c)", p=P),
                             allow_slow_non_contiguous=True).then_inc(s_dest[k], 16)

            load_rows(0, 0)
            load_rows(1, 1)
            load_rows(2, 0)
            load_dest(0, 0, 0)
            load_rows(3, 1)
            load_dest(1, 1, 0)
            with sp.Fori(2, BLOCKS // 2) as n:
                load_rows(2 * n, 0)
                load_dest(2 * n - 2, 0, n - 1)
                load_rows(2 * n + 1, 1)
                load_dest(2 * n - 1, 1, n - 1)
            load_dest(BLOCKS - 2, 0, BLOCKS // 2 - 1)
            load_dest(BLOCKS - 1, 1, BLOCKS // 2 - 1)

            for k in range(2):
                sp.wait_ge(s_part[k], 16 * HALVES * (BLOCKS // 2))
            ranks = parts.rearrange("(r t p) d -> p r t d", p=P, r=2)

            def part_load(g, k):
                wait(sp, s_sum, (g - CR + 1) * GROUP)
                a = k * 2 * GROUP * D
                for r in range(2):
                    sp.dma_start(pt[:, a + r * GROUP * D:a + (r + 1) * GROUP * D]
                                 .rearrange("p (t d) -> p t d", d=D),
                                 ranks[:, r, ds(g * GROUP, GROUP), :]).then_inc(s_pt[k], 16)

            for k in range(CR):
                part_load(k, k)
            with sp.Fori(1, GROUPS // CR) as n:
                for k in range(CR):
                    part_load(n * CR + k, k)

        @block.gpsimd
        def _(pool):
            nc.gpsimd.memset(adjt_i[:, :], 0).then_inc(s_adjz, 1)
            z3 = zeros[:, :].rearrange("p (h c) -> p h c", c=ROW32)
            nc.gpsimd.memset(z3[:, :, 0:D], 0)
            nc.gpsimd.memset(z3[:, :, D:ROW32], NOWHERE).then_inc(s_zeros, 1)

            w1_dram = w1.rearrange("x (c p) h -> p x c h", p=P)
            w2_dram = w2.rearrange("x (c p) h -> p x c h", p=P)

            def w_load(k):
                e, which = k % EXPERTS, k // EXPERTS
                src = (w1_dram, w2_dram)[which][:, e]
                a = (k % WRING) * WCOLS
                pool.dma_start(w_in[:, a:a + WCOLS].rearrange("p (c h) -> p c h", h=src.shape[2]),
                               src).then_inc(s_w[k % WRING], 16)

            for k in range(WRING):
                w_load(k)

            pool.wait_ge(s_const, 16 * N_CONST)
            m = const("mask")
            nc.gpsimd.tensor_copy(bpart[:, 0:D], bb[:, :]).then_inc(s_bias, 1)
            pool.wait_ge(s_bias, 1)
            nc.gpsimd.tensor_tensor(brest[:, 0:D], bb[:, :], bpart[:, 0:D], ALU.subtract).then_inc(s_bias, 1)
            pool.wait_ge(s_bias, 2)
            nc.gpsimd.tensor_copy(bpart[:, D:2 * D], brest[:, 0:D]).then_inc(s_bias, 1)
            pool.wait_ge(s_bias, 3)
            nc.gpsimd.tensor_tensor(brest[:, D:2 * D], brest[:, 0:D], bpart[:, D:2 * D],
                                    ALU.subtract).then_inc(s_bias, 1)
            pool.wait_ge(s_bias, 4)
            nc.gpsimd.tensor_copy(bpart[:, 2 * D:3 * D], brest[:, D:2 * D]).then_inc(s_bias, 1)
            pool.wait_ge(s_bias, 5)
            nc.gpsimd.tensor_scalar(bmask[:, 0:D], bpart[:, 0:D], m[:, 0:1], 1.0, ALU.mult, ALU.mult)
            nc.gpsimd.tensor_scalar(bmask[:, D:2 * D], bpart[:, D:2 * D], m[:, 1:2], 1.0,
                                    ALU.mult, ALU.mult).then_inc(s_bias, 1)
            pool.wait_ge(s_bias, 6)
            nc.gpsimd.tensor_tensor(bmask[:, 0:D], bmask[:, 0:D], bmask[:, D:2 * D], ALU.add).then_inc(s_bias, 1)
            pool.wait_ge(s_bias, 7)
            nc.gpsimd.tensor_scalar(bmask[:, D:2 * D], bpart[:, 2 * D:3 * D], m[:, 2:3], 1.0,
                                    ALU.mult, ALU.mult).then_inc(s_bias, 1)
            pool.wait_ge(s_bias, 8)
            nc.gpsimd.tensor_tensor(bias_rows[:, :], bmask[:, 0:D], bmask[:, D:2 * D], ALU.add).then_inc(s_bias, 1)

            for k in range(2 * EXPERTS):
                e, which = k % EXPERTS, k // EXPERTS
                a = (k % WRING) * WCOLS
                hi = (w1h, w2h)[which][:, e * WCOLS:(e + 1) * WCOLS]
                lo = (w1l, w2l)[which][:, e * WCOLS:(e + 1) * WCOLS]
                pool.wait_ge(s_w[k % WRING], 16 * (k // WRING + 1))
                wait(pool, s_wl, k)
                nc.gpsimd.tensor_scalar(w_sc[:, :], w_in[:, a:a + WCOLS], W_SCALE, 1.0,
                                        ALU.mult, ALU.mult).then_inc(s_wsc, 1)
                pool.wait_ge(s_wsc, k + 1)
                if k + WRING < 2 * EXPERTS:
                    w_load(k + WRING)
                nc.gpsimd.tensor_copy(hi, w_sc[:, :]).then_inc(s_wh, 1)
                pool.wait_ge(s_wh, k + 1)
                nc.gpsimd.tensor_tensor(lo, w_sc[:, :], hi, ALU.subtract).then_inc(s_wl, 1)

            def scatters(g, k):
                pool.wait_ge(s_place, g + 1)
                apart(pool, g)
                for j in range(GROUP):
                    slot = k * GROUP + j
                    for r in range(2):
                        pool.indirect_dma_start(
                            out=lists,
                            out_offset=bass.IndirectOffsetOnAxis(
                                ap=place[:, 2 * slot + r:2 * slot + r + 1], axis=0),
                            in_=row[:, slot * ROW32:(slot + 1) * ROW32], in_offset=None,
                        ).then_inc(s_scat[k], 16)

            NR = RING // GROUP
            PER = 16 * 2 * GROUP

            def scattered(n, k):
                pool.wait_ge(s_scat[k], PER * (n + 1))
                pool.sem_inc(s_free, 1)

            scatters(0, 0)
            for k in range(1, NR):
                scatters(k, k)
                scattered(0, k - 1)
            with pool.Fori(1, GROUPS // NR) as n:
                scatters(n * NR, 0)
                scattered(n - 1, NR - 1)
                for k in range(1, NR):
                    scatters(n * NR + k, k)
                    scattered(n, k - 1)
            pool.wait_ge(s_scat[NR - 1], PER * (GROUPS // NR))
            pool.sem_inc(s_listed, 1)

            def part_scatter(b, k, n):
                pool.wait_ge(s_dest[k], 16 * (n + 1))
                pool.wait_ge(s_y, b + 1)
                apart(pool, b)
                for h in range(HALVES):
                    i = k * HALVES + h
                    pool.indirect_dma_start(
                        out=parts,
                        out_offset=bass.IndirectOffsetOnAxis(ap=dest[:, i:i + 1], axis=0),
                        in_=y[:, i * D:(i + 1) * D], in_offset=None,
                        bounds_check=2 * TOKENS - 1, oob_is_err=False,
                    ).then_inc(s_part[k], 16)

            with pool.Fori(0, BLOCKS // 2) as n:
                part_scatter(2 * n, 0, n)
                part_scatter(2 * n + 1, 1, n)

        @block.scalar
        def _(act):
            act.dma_start(cf[:, :], consts_f).then_inc(s_const, 16)
            act.dma_start(ch[:, :], consts_h).then_inc(s_const, 16)
            act.dma_start(gw[:, :].rearrange("p (c o) -> p c o", o=D),
                          gnn_wt.rearrange("(c p) o -> p c o", p=P)).then_inc(s_const, 16)
            act.dma_start(bb[:, :], gnn_b.partition_broadcast(P)).then_inc(s_const, 16)
            act.dma_start(wg_f[:, :].rearrange("p (c e) -> p c e", e=EXPERTS),
                          wg.rearrange("(c p) e -> p c e", p=P)).then_inc(s_const, 16)
            act.dma_start(b1s[:, :], b1_t).then_inc(s_const, 16)
            act.dma_start(b2s[:, :], b2.rearrange("x e -> (x e)").partition_broadcast(P)).then_inc(s_const, 16)
            for j in range(GROUP - 1):
                act.dma_start(bg4[:, j * EXPERTS:(j + 1) * EXPERTS], bg.partition_broadcast(P)).then_inc(s_const, 16)
            act.dma_start(bg4[:, (GROUP - 1) * EXPERTS:], bg.partition_broadcast(P)).then_inc(s_const, 16)
            act.wait_ge(s_const, 16 * N_CONST)

            def step(s, j):
                tau = GROUP * s + j
                if j == 3 and has(s, s + 1):
                    g = s + 1
                    act.wait_ge(s_mv1, GROUP * (g + 1))
                    nc.scalar.activation(sd1[:, :], mv1[:, 1:2 * GROUP:2], ACT.Sqrt,
                                         bias=const("eps"), scale=1.0 / X_SCALE ** 2).then_inc(s_sd1, 1)
                if j == 2 and has(s, s - 1):
                    g = s - 1
                    act.wait_ge(s_mv2, GROUP * (g + 1))
                    nc.scalar.activation(sd2[:, :], mv2[:, 1:2 * GROUP:2], ACT.Sqrt,
                                         bias=const("eps"), scale=1.0 / X_SCALE ** 2).then_inc(s_sd2, 1)
                if has_tile(s, tau):
                    k = j % 2
                    src = X[:, ds(tau * D, D)]
                    act.wait_ge(s_nm1, s + 1)
                    wait(act, s_lo1, tau - 1)
                    wait(act, s_nbp, tau - 1)
                    nc.scalar.activation(xf1[:, k * D:(k + 1) * D], src, ACT.Identity,
                                         bias=nm1[:, ds(tau, 1)], scale=rs1[:, ds(tau, 1)])
                    nc.scalar.activation(xn1[:, k * 2 * D:k * 2 * D + D], src, ACT.Identity,
                                         bias=nm1[:, ds(tau, 1)], scale=rs1[:, ds(tau, 1)]).then_inc(s_hi1, 1)
                if has_tile(s, tau - 1):
                    k = (j + 1) % 2
                    act.wait_ge(s_nbp, tau)
                    wait(act, s_gnn, tau - 2)
                    nc.scalar.activation(z[:, k * 2 * D:(k + 1) * 2 * D], ps_nb[k][:, :], ACT.Copy,
                                         scale=1.0 / X_SCALE).then_inc(s_z, 1)
                if has_tile(s, tau - 7):
                    t = tau - 7
                    g, jj = (s - 2, j + 1) if j < 3 else (s - 1, 0)
                    k = (j + 1) % 2
                    src = X[:, ds(t * D, D)]
                    act.wait_ge(s_nm2, g + 1)
                    wait(act, s_lo2, t - 1)
                    wait(act, s_free, g - RING // GROUP + 1)
                    nc.scalar.activation(xf2[:, k * D:(k + 1) * D], src, ACT.Identity,
                                         bias=nm2[:, ds(t, 1)], scale=rs2[:, ds(t, 1)])
                    nc.scalar.activation(row16[:, ds((ring(g) + jj) * ROW16, D)], src, ACT.Identity,
                                         bias=nm2[:, ds(t, 1)], scale=rs2[:, ds(t, 1)]).then_inc(s_hi2, 1)

            for s in range(-1, 6):
                for j in range(GROUP):
                    step(s, j)
            with act.Fori(6, GROUPS - 1) as s:
                for j in range(GROUP):
                    step(s, j)
            for s in range(GROUPS - 1, GROUPS + 2):
                for j in range(GROUP):
                    step(s, j)

            def gelus(b, k):
                e = act.value_load(owner[0:1, ds(b, 1)], min_val=0, max_val=EXPERTS - 1)
                for c in range(HC):
                    act.wait_ge(s_hp, HC * b + c + 1)
                    wait(act, s_hl, HC * (b - 2) + c + 1)
                    a = (k * HC + c) * BLOCK
                    nc.scalar.activation(hf[:, a:a + BLOCK], ps_h[k][c][:, 0:BLOCK], ACT.Gelu,
                                         bias=b1s[:, ds(e * HC + c, 1)],
                                         scale=1.0 / (X_SCALE * W_SCALE)).then_inc(s_gelu, 1)

            act.wait_ge(s_tables, 2)
            gelus(0, 0)
            gelus(1, 1)
            with act.Fori(1, BLOCKS // 2) as n:
                gelus(2 * n, 0)
                gelus(2 * n + 1, 1)
            nc.scalar.activation(ge[:, :], gap[:, :], ACT.Exp).then_inc(s_ge, 1)

            with act.Fori(0, GROUPS) as g:
                act.wait_ge(s_sum, GROUP * (g + 1))
                act.dma_start(out_dram[:, ds(g * GROUP, GROUP), :],
                              X3[:, ds(g * GROUP, GROUP), :]).then_inc(s_out, 16)
            act.wait_ge(s_out, 16 * GROUPS)

        @block.tensor
        def _(pe):
            mm = nc.tensor.matmul
            pe.wait_ge(s_const, 16 * N_CONST)
            pe.wait_ge(s_nb, 1)
            mm(ps_place[:, 0:P], ones, nb[:, 0:P], start=True, stop=True).then_inc(s_degp, 1)
            pe.wait_ge(s_deg, 1)
            pe.wait_ge(s_nb, 2)
            pe.wait_ge(s_bias, 9)
            pe.wait_ge(s_wgr, 1)

            def step(s, j):
                tau = GROUP * s + j
                if has_tile(s, tau):
                    k = j % 2
                    pe.wait_ge(s_lo1, tau + 1)
                    wait(pe, s_z, tau - 1)
                    for c in range(DC):
                        for part in range(2):
                            a = k * 2 * D + part * D + c * P
                            last = mm(ps_nb[k][:, c * 2 * P:(c + 1) * 2 * P], xn1[:, a:a + P], nb[:, :],
                                      start=part == 0, stop=part == 1)
                    last.then_inc(s_nbp, 1)
                if has_tile(s, tau - 1):
                    k = (j + 1) % 2
                    o = ps_gnn[k][:, 0:D]
                    pe.wait_ge(s_z, tau)
                    wait(pe, s_x1, tau - 2)
                    mm(o, deg_rows[:, :], bias_rows[:, :], start=True, stop=False)
                    for c in range(DC):
                        a = k * 2 * D + c * 2 * P
                        mm(o, z[:, a:a + P], gw[:, (DC + c) * D:(DC + c + 1) * D], start=False, stop=False)
                        last = mm(o, z[:, a + P:a + 2 * P], gw[:, c * D:(c + 1) * D],
                                  start=False, stop=c == DC - 1)
                    last.then_inc(s_gnn, 1)
                if j == 0 and has(s, s - 4):
                    g = s - 4
                    pe.wait_ge(s_chose, g + 1)
                    n = EXPERTS
                    mm(ps_place[:, 0:GROUP * n], below, chose[:, :], start=True, stop=False)
                    for i in range(GROUP):
                        mm(ps_place[:, i * n:(i + 1) * n], ones, before[:, :], start=False, stop=False)
                        for q in range(i):
                            last = mm(ps_place[:, i * n:(i + 1) * n], ones, chose[:, q * n:(q + 1) * n],
                                      start=False, stop=(i, q) == (GROUP - 1, GROUP - 2))
                    last.then_inc(s_pp, 1)
                if has_tile(s, tau - 11):
                    t = tau - 11
                    g, jj = (s - 3, j + 1) if j < 3 else (s - 2, 0)
                    pe.wait_ge(s_gT[jj], 16 * (g + 1))
                    wait(pe, s_score, g)
                    o = ps_score[:, jj * EXPERTS:(jj + 1) * EXPERTS]
                    for c in range(DC):
                        hi = gT[:, jj * 2 * D + c * P:jj * 2 * D + (c + 1) * P]
                        lo = gT[:, jj * 2 * D + D + c * P:jj * 2 * D + D + (c + 1) * P]
                        wh = wg_h[:, c * EXPERTS:(c + 1) * EXPERTS]
                        wl = wg_h[:, (DC + c) * EXPERTS:(DC + c + 1) * EXPERTS]
                        mm(o, hi, wl, start=c == 0, stop=False)
                        mm(o, lo, wh, start=False, stop=False)
                        last = mm(o, hi, wh, start=False, stop=c == DC - 1)
                    last.then_inc(s_sp, 1)

            for s in range(0, 4):
                for j in range(GROUP):
                    step(s, j)
            with pe.Fori(4, GROUPS) as s:
                for j in range(GROUP):
                    step(s, j)
            for s in range(GROUPS, GROUPS + 4):
                for j in range(GROUP):
                    step(s, j)
            pe.wait_ge(s_place, GROUPS)
            mm(ps_place[:, 0:EXPERTS], ones, before[:, :], start=True, stop=True).then_inc(s_cntp, 1)

            def hidden(b, k, n):
                w0 = pe.value_load(weights_at[0:1, ds(b, 1)], min_val=0, max_val=(EXPERTS - 1) * WCOLS)
                pe.wait_ge(s_xT[k], 16 * (n + 1))
                for h in range(HC):
                    wait(pe, s_gelu, HC * (b - 2) + h + 1)
                    o = ps_h[k][h][:, 0:BLOCK]
                    for c in range(DC):
                        a = k * 2 * DC * BLOCK + c * BLOCK
                        hi, lo = xT[:, a:a + BLOCK], xT[:, a + DC * BLOCK:a + (DC + 1) * BLOCK]
                        w = ds(w0 + (c * H + h * P), P)
                        mm(o, w1l[:, w], hi, start=c == 0, stop=False)
                        mm(o, w1h[:, w], lo, start=False, stop=False)
                        last = mm(o, w1h[:, w], hi, start=False, stop=c == DC - 1)
                    last.then_inc(s_hp, 1)

            def output(b, k):
                w0 = pe.value_load(weights_at[0:1, ds(b, 1)], min_val=0, max_val=(EXPERTS - 1) * WCOLS)
                wait(pe, s_y, b - 1)
                for h in range(HC):
                    pe.wait_ge(s_hl, HC * b + h + 1)
                    w = ds(w0 + h * D, D)
                    for left, right in ((hl, w2h), (hh, w2h), (hh, w2l)):
                        for m in range(HALVES):
                            a = (k * HC + h) * BLOCK + m * P
                            last = mm(ps_y[k][:, m * D:(m + 1) * D], left[:, a:a + P], right[:, w],
                                      start=(h, m) == (0, 0) and left is hl,
                                      stop=(h, m) == (HC - 1, 1) and right is w2l,
                                      skip_group_check=True)
                last.then_inc(s_yp, 1)

            pe.wait_ge(s_tables, 2)
            pe.wait_ge(s_wl, 2 * EXPERTS)
            hidden(0, 0, 0)
            hidden(1, 1, 0)
            output(0, 0)
            hidden(2, 0, 1)
            output(1, 1)
            hidden(3, 1, 1)
            output(2, 0)
            with pe.Fori(2, BLOCKS // 2) as n:
                hidden(2 * n, 0, n)
                output(2 * n - 1, 1)
                hidden(2 * n + 1, 1, n)
                output(2 * n, 0)
            output(BLOCKS - 1, 1)

        @block.vector
        def _(dve):
            v = nc.vector
            dve.wait_ge(s_const, 16 * N_CONST)
            dve.wait_ge(s_adj, 64)
            v.tensor_copy(nb[:, 0:P], adjt_i[:, :]).then_inc(s_nb, 1)
            v.tensor_copy(adj_f[:, :], adj_i[:, :]).then_inc(s_setup, 1)
            v.tensor_scalar(wg_s[:, :], wg_f[:, :], W_SCALE, None, ALU.mult).then_inc(s_setup, 1)
            v.memset(before[:, :], 0.0)
            dve.wait_ge(s_setup, 1)
            v.tensor_reduce(deg[:, :], adj_f[:, :], AX_X, ALU.add).then_inc(s_setup, 1)
            NW = DC * EXPERTS
            dve.wait_ge(s_setup, 2)
            v.tensor_copy(wg_h[:, 0:NW], wg_s[:, :]).then_inc(s_setup, 1)
            dve.wait_ge(s_setup, 3)
            v.tensor_scalar(nb[:, P:2 * P], const("ident"), deg[:, 0:1], None, ALU.mult).then_inc(s_nb, 1)
            dve.wait_ge(s_setup, 4)
            v.tensor_tensor(wg_h[:, NW:2 * NW], wg_s[:, :], wg_h[:, 0:NW], ALU.subtract).then_inc(s_wgr, 1)
            dve.wait_ge(s_degp, 1)
            v.tensor_scalar(deg_rows[:, :], ps_place[:, 0:P], const("mask3"), None, ALU.mult).then_inc(s_deg, 1)

            def step(s, j):
                tau = GROUP * s + j
                if j == 3 and has(s, s - 3):
                    g = s - 3
                    dve.wait_ge(s_sp, GROUP * (g + 1))
                    v.scalar_tensor_tensor(
                        out=score[:, :], in0=ps_score[:, 0:GROUP * EXPERTS],
                        scalar=1.0 / (X_SCALE * W_SCALE), in1=bg4[:, :],
                        op0=ALU.mult, op1=ALU.add).then_inc(s_score, 1)
                if has_tile(s, tau):
                    k = j % 2
                    dve.wait_ge(s_hi1, tau + 1)
                    v.tensor_tensor(xn1[:, k * 2 * D + D:(k + 1) * 2 * D], xf1[:, k * D:(k + 1) * D],
                                    xn1[:, k * 2 * D:k * 2 * D + D], ALU.subtract).then_inc(s_lo1, 1)
                if has_tile(s, tau - 2):
                    k = j % 2
                    xt = X[:, ds((tau - 2) * D, D)]
                    dve.wait_ge(s_gnn, tau - 1)
                    v.tensor_tensor(xt, ps_gnn[k][:, 0:D], xt, ALU.add).then_inc(s_x1, 1)
                if j == 3 and has(s, s + 1):
                    g = s + 1
                    dve.wait_ge(s_sd1, g + 1)
                    v.reciprocal(rs1[:, ds(g * GROUP, GROUP)], sd1[:, :]).then_inc(s_rs1, 1)
                if j == 2 and has(s, s - 1):
                    g = s - 1
                    dve.wait_ge(s_sd2, g + 1)
                    v.reciprocal(rs2[:, ds(g * GROUP, GROUP)], sd2[:, :]).then_inc(s_rs2, 1)
                if has_tile(s, tau + 5):
                    g, jj = (s + 1, j + 1) if j < 3 else (s + 2, 0)
                    dve.wait_ge(s_x, 16 * (g + 1))
                    v.bn_stats(stat1[:, (jj % 2) * 6:(jj % 2) * 6 + 6],
                               X[:, ds((tau + 5) * D, D)]).then_inc(s_bn1, 1)
                if j == 3 and has(s, s + 1):
                    g = s + 1
                    dve.wait_ge(s_rs1, g + 1)
                    v.scalar_tensor_tensor(
                        out=nm1[:, ds(g * GROUP, GROUP)], in0=mv1[:, 0:2 * GROUP:2], scalar=-1.0,
                        in1=rs1[:, ds(g * GROUP, GROUP)], op0=ALU.mult, op1=ALU.mult).then_inc(s_nm1, 1)
                if has_tile(s, tau - 2):
                    jj = (j + 2) % 4
                    dve.wait_ge(s_x1, tau - 1)
                    apart(dve, s)
                    v.bn_stats(stat2[:, (jj % 2) * 6:(jj % 2) * 6 + 6],
                               X[:, ds((tau - 2) * D, D)]).then_inc(s_bn2, 1)
                if j == 2 and has(s, s - 1):
                    g = s - 1
                    dve.wait_ge(s_rs2, g + 1)
                    v.scalar_tensor_tensor(
                        out=nm2[:, ds(g * GROUP, GROUP)], in0=mv2[:, 0:2 * GROUP:2], scalar=-1.0,
                        in1=rs2[:, ds(g * GROUP, GROUP)], op0=ALU.mult, op1=ALU.mult).then_inc(s_nm2, 1)
                if has_tile(s, tau + 5):
                    jj = (j + 1) % 4
                    if j == 3:
                        wait(dve, s_nm1, s + 2)
                    dve.wait_ge(s_bn1, tau + 6)
                    apart(dve, s)
                    v.bn_aggr(mv1[:, 2 * jj:2 * jj + 2], stat1[:, (jj % 2) * 6:(jj % 2) * 6 + 6]).then_inc(s_mv1, 1)
                if has_tile(s, tau - 8):
                    t = tau - 8
                    g, jj = s - 2, j
                    k = j % 2
                    a = (ring(g) + jj) * ROW16
                    dve.wait_ge(s_hi2, t + 1)
                    v.tensor_tensor(row16[:, ds(a + D, D)], xf2[:, k * D:(k + 1) * D],
                                    row16[:, ds(a, D)], ALU.subtract).then_inc(s_lo2, 1)
                if has_tile(s, tau - 2):
                    jj = (j + 2) % 4
                    if j == 2:
                        wait(dve, s_nm2, s)
                    dve.wait_ge(s_bn2, tau - 1)
                    apart(dve, s)
                    v.bn_aggr(mv2[:, 2 * jj:2 * jj + 2], stat2[:, (jj % 2) * 6:(jj % 2) * 6 + 6]).then_inc(s_mv2, 1)
                if j == 3 and has(s, s - 3):
                    choose(s - 3)
                if j == 1 and has(s, s - 4):
                    find_places(s - 4)

            def choose(g):
                n = EXPERTS
                dve.wait_ge(s_score, g + 1)
                apart(dve, g)
                for i in range(GROUP):
                    last = v.max(best[:, 8 * i:8 * i + 8], score[:, n * i:n * (i + 1)])
                last.then_inc(s_route, 1)
                dve.wait_ge(s_route, 5 * g + 1)
                apart(dve, g)
                for i in range(GROUP):
                    last = v.max_index(best_i[:, 8 * i:8 * i + 8], best[:, 8 * i:8 * i + 8],
                                       score[:, n * i:n * (i + 1)])
                last.then_inc(s_route, 1)
                b3 = best[:, :].rearrange("p (t k) -> p t k", k=8)
                v.tensor_tensor(gap[:, ds(g * GROUP, GROUP)], b3[:, :, 1], b3[:, :, 0], ALU.subtract)
                dve.wait_ge(s_route, 5 * g + 2)
                v.tensor_copy(best_f[:, :].rearrange("p (t r) -> p t r", r=2),
                              best_i[:, :].rearrange("p (t k) -> p t k", k=8)[:, :, 0:2]).then_inc(s_route, 1)
                dve.wait_ge(s_route, 5 * g + 3)
                v.tensor_tensor(chose2[:, :].rearrange("p (q e) -> p q e", e=n),
                                const("iota").rearrange("p (q e) -> p q e", e=n),
                                best_f[:, :].unsqueeze(2).to_broadcast([P, 2 * GROUP, n]),
                                ALU.is_equal).then_inc(s_route, 1)
                dve.wait_ge(s_route, 5 * g + 4)
                c4 = chose2[:, :].rearrange("p (t r e) -> p t r e", r=2, e=n)
                v.tensor_tensor(chose[:, :].rearrange("p (t e) -> p t e", e=n),
                                c4[:, :, 0, :], c4[:, :, 1, :], ALU.add).then_inc(s_chose, 1)
                v.scalar_tensor_tensor(
                    out=row[:, ds(ring(g) * ROW32, GROUP * ROW32)]
                    .rearrange("p (t c) -> p t c", c=ROW32)[:, :, D:ROW32],
                    in0=c4[:, :, 1, :], scalar=float(TOKENS),
                    in1=const_token(g).unsqueeze(2).to_broadcast([P, GROUP, n]),
                    op0=ALU.mult, op1=ALU.add)
                dve.wait_ge(s_chose, g + 1)
                v.tensor_reduce(chose_g[:, :], chose[:, :].rearrange("p (t e) -> p e t", e=n),
                                AX_X, ALU.add).then_inc(s_route, 1)

            def const_token(g):
                a, _ = cols["token"]
                return cf[:, ds(g * GROUP + a, GROUP)]

            def find_places(g):
                n = EXPERTS
                dve.wait_ge(s_pp, g + 1)
                v.tensor_tensor(place_e[:, :], ps_place[:, 0:GROUP * n], const("list_start"),
                                ALU.add).then_inc(s_step, 1)
                dve.wait_ge(s_route, 5 * g + 5)
                v.tensor_tensor(before[:, :], before[:, :], chose_g[:, :], ALU.add)
                dve.wait_ge(s_step, 3 * g + 1)
                v.tensor_tensor(place2[:, :].rearrange("p (t r e) -> p t r e", r=2, e=n),
                                chose2[:, :].rearrange("p (t r e) -> p t r e", r=2, e=n),
                                place_e[:, :].rearrange("p (t e) -> p t e", e=n).unsqueeze(2)
                                .to_broadcast([P, GROUP, 2, n]), ALU.mult).then_inc(s_step, 1)
                dve.wait_ge(s_step, 3 * g + 2)
                v.tensor_reduce(place_f[:, :], place2[:, :].rearrange("p (q e) -> p q e", e=n), AX_X,
                                ALU.add).then_inc(s_step, 1)
                dve.wait_ge(s_step, 3 * g + 3)
                v.tensor_copy(place[:, ds(2 * ring(g), 2 * GROUP)], place_f[:, :]).then_inc(s_place, 1)

            for s in range(-2, 4):
                for j in range(GROUP):
                    step(s, j)
            with dve.Fori(4, GROUPS - 2) as s:
                for j in range(GROUP):
                    step(s, j)
            for s in range(GROUPS - 2, GROUPS + 4):
                for j in range(GROUP):
                    step(s, j)

            n, most = EXPERTS, TOKENS // BLOCK
            dve.wait_ge(s_cntp, 1)
            v.tensor_copy(count[:, :], ps_place[:, 0:n]).then_inc(s_tab, 1)
            dve.wait_ge(s_tab, 1)
            v.tensor_tensor(list_end[:, :], count[:, :], const("list_start")[:, 0:n], ALU.add).then_inc(s_tables, 1)
            v.tensor_tensor(full[:, :].rearrange("p (e k) -> p e k", k=most),
                            count[:, :].unsqueeze(2).to_broadcast([P, n, most]),
                            const("whole").rearrange("p (e k) -> p e k", k=most), ALU.is_gt).then_inc(s_tab, 1)
            dve.wait_ge(s_tab, 2)
            v.tensor_reduce(nblk[:, :], full[:, :].rearrange("p (e k) -> p e k", k=most), AX_X,
                            ALU.add).then_inc(s_tab, 1)
            dve.wait_ge(s_tab, 3)
            v.tensor_tensor_scan(cum[:, :], nblk[:, :], const("zero"), 0.0, ALU.add, ALU.add).then_inc(s_tab, 1)
            v.tensor_scalar(skip[:, :], nblk[:, :], -float(BLOCK), float(LIST_ROWS), ALU.mult,
                            ALU.add).then_inc(s_tab, 1)
            dve.wait_ge(s_tab, 5)
            p3 = passed[:, :].rearrange("p (b e) -> p b e", e=n)
            v.tensor_tensor(p3, cum[:, :].unsqueeze(1).to_broadcast([P, BLOCKS, n]),
                            const("block").unsqueeze(2).to_broadcast([P, BLOCKS, n]),
                            ALU.is_le).then_inc(s_tab, 1)
            dve.wait_ge(s_tab, 6)
            v.tensor_tensor(skipped[:, :].rearrange("p (b e) -> p b e", e=n), p3,
                            skip[:, :].unsqueeze(1).to_broadcast([P, BLOCKS, n]), ALU.mult).then_inc(s_tab, 1)
            v.tensor_reduce(owner_f[:, :], p3, AX_X, ALU.add).then_inc(s_tab, 1)
            dve.wait_ge(s_tab, 7)
            v.tensor_reduce(start_f[:, 0:BLOCKS], skipped[:, :].rearrange("p (b e) -> p b e", e=n), AX_X,
                            ALU.add).then_inc(s_tab, 1)
            dve.wait_ge(s_tab, 8)
            v.tensor_scalar(owner[:, :], owner_f[:, :], float(EXPERTS - 1), None, ALU.min).then_inc(s_tab, 1)
            dve.wait_ge(s_tab, 10)
            v.tensor_scalar(weights_at[:, :], owner[:, :], float(WCOLS), None, ALU.mult).then_inc(s_tab, 1)
            v.tensor_tensor(start_f[:, BLOCKS:2 * BLOCKS], start_f[:, 0:BLOCKS], const("block_row"),
                            ALU.add).then_inc(s_tab, 1)
            dve.wait_ge(s_tab, 12)
            v.tensor_scalar(start[:, :], start_f[:, BLOCKS:2 * BLOCKS], float(ZERO_LIST), None,
                            ALU.min).then_inc(s_tables, 1)

            def cut(b, k):
                for c in range(HC):
                    a = (k * HC + c) * BLOCK
                    dve.wait_ge(s_gelu, HC * b + c + 1)
                    wait(dve, s_yp, b - 1)
                    v.tensor_scalar(hh[:, a:a + BLOCK], hf[:, a:a + BLOCK], H_SCALE, None,
                                    ALU.mult).then_inc(s_hh, 1)
                    dve.wait_ge(s_hh, HC * b + c + 1)
                    v.scalar_tensor_tensor(out=hl[:, a:a + BLOCK], in0=hf[:, a:a + BLOCK],
                                           scalar=H_SCALE, in1=hh[:, a:a + BLOCK],
                                           op0=ALU.mult, op1=ALU.subtract).then_inc(s_hl, 1)

            def results(b, k, n):
                e = dve.value_load(owner[0:1, ds(b, 1)], min_val=0, max_val=EXPERTS - 1)
                dve.wait_ge(s_yp, b + 1)
                wait(dve, s_part[k], 16 * HALVES * n)
                a = k * HALVES * D
                v.scalar_tensor_tensor(
                    out=y[:, a:a + HALVES * D].rearrange("p (h d) -> p h d", d=D),
                    in0=ps_y[k][:, :].rearrange("p (h d) -> p h d", d=D),
                    scalar=1.0 / (H_SCALE * W_SCALE),
                    in1=b2s[:, ds(e * D, D)].unsqueeze(1).to_broadcast([P, HALVES, D]),
                    op0=ALU.mult, op1=ALU.add).then_inc(s_y, 1)

            dve.wait_ge(s_tables, 2)
            cut(0, 0)
            cut(1, 1)
            results(0, 0, 0)
            cut(2, 0)
            results(1, 1, 0)
            cut(3, 1)
            results(2, 0, 1)
            with dve.Fori(2, BLOCKS // 2) as n:
                cut(2 * n, 0)
                results(2 * n - 1, 1, n - 1)
                cut(2 * n + 1, 1)
                results(2 * n, 0, n)
            results(BLOCKS - 1, 1, BLOCKS // 2 - 1)

            dve.wait_ge(s_ge, 1)
            v.tensor_scalar(gd[:, :], ge[:, :], 1.0, None, ALU.add).then_inc(s_gate, 1)
            dve.wait_ge(s_gate, 1)
            v.reciprocal(g0[:, :], gd[:, :]).then_inc(s_gate, 1)
            dve.wait_ge(s_gate, 2)
            v.tensor_tensor(g1[:, :], g0[:, :], ge[:, :], ALU.mult).then_inc(s_gate, 1)
            dve.wait_ge(s_gate, 3)

            def sums(g, k, n):
                dve.wait_ge(s_pt[k], 32 * (n + 1))
                for r, gate in ((0, g0), (1, g1)):
                    for j in range(GROUP):
                        a = (k * 2 + r) * GROUP * D + j * D
                        xt = X[:, ds((g * GROUP + j) * D, D)]
                        if r == 1:
                            dve.wait_ge(s_sum0, GROUP * g + j + 1)
                        v.scalar_tensor_tensor(
                            out=xt, in0=pt[:, a:a + D], scalar=gate[:, ds(g * GROUP + j, 1)], in1=xt,
                            op0=ALU.mult, op1=ALU.add).then_inc(s_sum0 if r == 0 else s_sum, 1)

            with dve.Fori(0, GROUPS // CR) as n:
                for k in range(CR):
                    sums(n * CR + k, k, n)


def host_constants(tokens, experts, group, block):
    import numpy as np

    p = 128
    tiles = tokens // p
    blocks = 2 * tokens // block + experts
    list_rows = tokens + block

    def rows(a):
        return np.broadcast_to(np.asarray(a, np.float32).reshape(1, -1), (p, np.size(a)))

    parts = [
        np.eye(p, dtype=np.float32),
        rows(np.tile(np.arange(experts), 2 * group)),
        rows(np.tile(np.arange(experts) * list_rows, group)),
        (np.arange(tiles)[None, :] * p + np.arange(p)[:, None]).astype(np.float32),
        (np.arange(p)[:, None] == np.arange(3)[None, :]).astype(np.float32),
        (np.arange(p)[:, None] < 3).astype(np.float32),
        rows(np.arange(blocks) * block),
        rows(np.arange(blocks)),
        rows(np.tile(np.arange(tokens // block) * block, experts)),
        rows(np.zeros(experts)),
        np.full((p, 1), 1e-5 / 256.0 ** 2, np.float32),
    ]
    below = (np.arange(p)[:, None] < np.arange(p)[None, :]).astype(np.float16)
    return (np.ascontiguousarray(np.concatenate(parts, 1)),
            np.ascontiguousarray(np.concatenate([below, np.ones((p, p), np.float16)], 1)))


def kernel(x, adj, L0_gnn_W, L0_gnn_b, L0_ffn_Wg, L0_ffn_bg, L0_ffn_W1, L0_ffn_b1, L0_ffn_W2, L0_ffn_b2):
    import concourse.bacc as bacc
    import numpy as np
    from concourse import mybir
    from concourse.bass_utils import run_bass_kernel_spmd

    x = np.asarray(x)
    w1 = np.asarray(L0_ffn_W1)
    experts, _, h = w1.shape
    consts_f, consts_h = host_constants(x.shape[0] * x.shape[1], experts, 4, 256)
    adj = np.asarray(adj)
    b1 = np.asarray(L0_ffn_b1)
    arrays = {
        "x": x, "adj": adj, "adj_t": adj.T, "gnn_wt": np.asarray(L0_gnn_W).T, "gnn_b": np.asarray(L0_gnn_b),
        "wg": np.asarray(L0_ffn_Wg), "bg": np.asarray(L0_ffn_bg), "w1": w1,
        "b1_t": b1.reshape(experts, h // 128, 128).transpose(2, 0, 1).reshape(128, -1),
        "w2": np.asarray(L0_ffn_W2), "b2": np.asarray(L0_ffn_b2),
        "consts_f": consts_f, "consts_h": consts_h,
    }
    arrays = {k: np.ascontiguousarray(a) for k, a in arrays.items()}
    nc = bacc.Bacc("TRN2", target_bir_lowering=False, num_devices=1)
    args = {k: nc.dram_tensor(f"in_{k}", a.shape, mybir.dt.from_np(a.dtype), kind="ExternalInput").ap()
            for k, a in arrays.items()}
    out = nc.dram_tensor("out_x", x.shape, mybir.dt.float32, kind="ExternalOutput").ap()
    build(nc, **args, out=out)
    result = run_bass_kernel_spmd(nc, [{f"in_{k}": a for k, a in arrays.items()}], core_ids=[0])
    return result.results[0]["out_x"]
```

```python
def build(nc, x, adj, adj_t, gnn_wt, gnn_b, wg, bg, w1, b1_t, w2, b2, consts_f, consts_h, out):
    from contextlib import ExitStack

    import concourse.bass as bass
    from concourse import mybir

    F32, F16, BF16 = mybir.dt.float32, mybir.dt.float16, mybir.dt.bfloat16
    I32, U32 = mybir.dt.int32, mybir.dt.uint32
    ALU = mybir.AluOpType
    ACT = mybir.ActivationFunctionType
    AX_X = mybir.AxisListType.X
    ds = bass.ds

    P = 128
    B, NODES, D = x.shape
    TOKENS = B * NODES
    TILES = TOKENS // P
    EXPERTS, _, H = w1.shape
    GROUP = 4
    GROUPS = TILES // GROUP
    DC, HC = D // P, H // P
    EPS = 1e-5
    X_SCALE = 256.0
    W_SCALE = 1024.0
    H_SCALE = 64.0
    BLOCK = 256
    HALVES = BLOCK // P
    LIST_ROWS = TOKENS + BLOCK
    BLOCKS = 2 * TOKENS // BLOCK + EXPERTS
    ZERO_LIST = EXPERTS * LIST_ROWS
    ROWS = ZERO_LIST + BLOCK
    ROW32 = D + EXPERTS
    ROW16 = 2 * ROW32
    NOWHERE = 1 << 20
    RING = 4 * GROUP
    WCOLS = DC * H
    WRING = 4
    AHEAD = 7

    col = 0
    cols = {}
    for name, n in (("ident", P), ("iota", 2 * GROUP * EXPERTS), ("list_start", GROUP * EXPERTS),
                    ("token", TILES), ("mask", 3), ("mask3", 1), ("block_row", BLOCKS), ("block", BLOCKS),
                    ("whole", EXPERTS * (TOKENS // BLOCK)), ("zero", EXPERTS), ("eps", 1)):
        cols[name] = (col, n)
        col += n
    NCF = col

    lists = nc.dram_tensor("lists", [ROWS, ROW32], I32).ap()
    lists16 = lists.bitcast(F16)
    parts = nc.dram_tensor("parts", [2 * TOKENS, D], F32).ap()

    with ExitStack() as ctx:
        def sb(name, shape, dt):
            return ctx.enter_context(nc.sbuf_tensor(name, shape, dt))

        def sem(name):
            return ctx.enter_context(nc.semaphore(name))

        bank = [ctx.enter_context(nc.psum_tensor(f"bank{i}", [P, 512], F32)) for i in range(8)]
        ps_nb = bank[0:2]
        ps_gnn = bank[2:4]
        ps_score = bank[4]
        ps_place = bank[5]
        ps_h = [bank[0:3], bank[3:6]]
        ps_y = bank[6:8]

        X = sb("X", [P, TILES * D], F32)
        cf = sb("cf", [P, NCF], F32)
        ch = sb("ch", [P, 2 * P], F16)

        def const(name):
            a, n = cols[name]
            return cf[:, a:a + n]

        below, ones = ch[:, 0:P], ch[:, P:2 * P]

        adj_i = sb("adj_i", [P, NODES], I32)
        adj_f = sb("adj_f", [P, NODES], F32)
        adjt_i = sb("adjt_i", [P, P], I32)
        deg = sb("deg", [P, 1], F32)
        nb = sb("nb", [P, 2 * P], F16)
        deg_rows = sb("deg_rows", [P, P], F16)
        gw = sb("gw", [P, 2 * DC * D], F32)
        bias_rows = sb("bias_rows", [P, D], BF16)
        bb = sb("bb", [P, D], F32)
        bpart = sb("bpart", [P, 3 * D], BF16)
        brest = sb("brest", [P, 2 * D], F32)
        bmask = sb("bmask", [P, 2 * D], F32)
        wg_f = sb("wg_f", [P, DC * EXPERTS], F32)
        wg_s = sb("wg_s", [P, DC * EXPERTS], F32)
        wg_h = sb("wg_h", [P, 2 * DC * EXPERTS], F16)
        bg4 = sb("bg4", [P, GROUP * EXPERTS], F32)

        stat1 = sb("stat1", [P, 2 * 6], F32)
        stat2 = sb("stat2", [P, 2 * 6], F32)
        mv1 = sb("mv1", [P, GROUP * 2], F32)
        mv2 = sb("mv2", [P, GROUP * 2], F32)
        sd1 = sb("sd1", [P, GROUP], F32)
        sd2 = sb("sd2", [P, GROUP], F32)
        rs1 = sb("rs1", [P, TILES], F32)
        nm1 = sb("nm1", [P, TILES], F32)
        rs2 = sb("rs2", [P, TILES], F32)
        nm2 = sb("nm2", [P, TILES], F32)
        mvc1 = sb("mvc1", [P, GROUP * 2], F32)
        mvc2 = sb("mvc2", [P, GROUP * 2], F32)
        xf1 = sb("xf1", [P, GROUP * D], F32)
        xn1 = sb("xn1", [P, GROUP * 2 * D], F16)
        z = sb("z", [P, 2 * 2 * D], F32)
        xf2 = sb("xf2", [P, 2 * D], F32)
        row = sb("row", [P, RING * ROW32], I32)
        row16 = row[:, :].bitcast(F16)
        gT = sb("gT", [P, GROUP * 2 * DC * P], F16)
        score = sb("score", [P, GROUP * EXPERTS], F32)
        best = sb("best", [P, GROUP * 8], F32)
        best_i = sb("best_i", [P, GROUP * 8], U32)
        best_f = sb("best_f", [P, GROUP * 2], F32)
        chose2 = sb("chose2", [P, GROUP * 2 * EXPERTS], F32)
        chose = sb("chose", [P, GROUP * EXPERTS], F16)
        chose_g = sb("chose_g", [P, EXPERTS], F32)
        before = sb("before", [P, EXPERTS], F16)
        place_e = sb("place_e", [P, GROUP * EXPERTS], F32)
        place2 = sb("place2", [P, GROUP * 2 * EXPERTS], F32)
        place_f = sb("place_f", [P, GROUP * 2], F32)
        place = sb("place", [P, RING * 2], I32)
        gap = sb("gap", [P, TILES], F32)

        w_in = sb("w_in", [P, WRING * WCOLS], F32)
        w_sc = sb("w_sc", [P, WCOLS], F32)
        cuts = sb("cuts", [P, 4 * EXPERTS * WCOLS], F16)
        w1h, w1l, w2h, w2l = (cuts[:, i * EXPERTS * WCOLS:(i + 1) * EXPERTS * WCOLS] for i in range(4))
        b1s = sb("b1s", [P, EXPERTS * HC], F32)
        b2s = sb("b2s", [P, EXPERTS * D], F32)

        count = sb("count", [P, EXPERTS], F32)
        full = sb("full", [P, EXPERTS * (TOKENS // BLOCK)], F32)
        nblk = sb("nblk", [P, EXPERTS], F32)
        cum = sb("cum", [P, EXPERTS], F32)
        skip = sb("skip", [P, EXPERTS], F32)
        passed = sb("passed", [P, BLOCKS * EXPERTS], F32)
        skipped = sb("skipped", [P, BLOCKS * EXPERTS], F32)
        owner_f = sb("owner_f", [P, BLOCKS], F32)
        start_f = sb("start_f", [P, 2 * BLOCKS], F32)
        owner = sb("owner", [P, BLOCKS], I32)
        weights_at = sb("weights_at", [P, BLOCKS], I32)
        start = sb("start", [P, BLOCKS], I32)
        list_end = sb("list_end", [P, EXPERTS], I32)
        zeros = sb("zeros", [P, HALVES * ROW32], I32)

        xT = sb("xT", [P, 2 * 2 * DC * BLOCK], F16)
        dest = sb("dest", [P, 2 * HALVES], I32)
        HCOLS = 2 * HC * BLOCK
        hf = w_in[:, 0:HCOLS]
        hh = w_in[:, HCOLS:HCOLS + HCOLS // 2].bitcast(F16)
        hl = w_in[:, HCOLS + HCOLS // 2:2 * HCOLS].bitcast(F16)
        y = sb("y", [P, 2 * HALVES * D], F32)

        CR = 4
        pt = cuts[:, 0:2 * CR * 2 * GROUP * D].bitcast(F32)
        ge = sb("ge", [P, TILES], F32)
        gd = sb("gd", [P, TILES], F32)
        g0 = sb("g0", [P, TILES], F32)
        g1 = sb("g1", [P, TILES], F32)

        s_const = sem("s_const")
        s_adjz = sem("s_adjz")
        s_adj = sem("s_adj")
        s_setup = sem("s_setup")
        s_nb = sem("s_nb")
        s_degp = sem("s_degp")
        s_deg = sem("s_deg")
        s_bias = sem("s_bias")
        s_wgr = sem("s_wgr")
        s_x = sem("s_x")
        s_bn1 = sem("s_bn1")
        s_mv1 = sem("s_mv1")
        s_mvc1 = sem("s_mvc1")
        s_mvc2 = sem("s_mvc2")
        s_sd1 = sem("s_sd1")
        s_rs1 = sem("s_rs1")
        s_nm1 = sem("s_nm1")
        s_bn2 = sem("s_bn2")
        s_mv2 = sem("s_mv2")
        s_sd2 = sem("s_sd2")
        s_rs2 = sem("s_rs2")
        s_nm2 = sem("s_nm2")
        s_hi1 = sem("s_hi1")
        s_lo1 = sem("s_lo1")
        s_nbp = sem("s_nbp")
        s_z = sem("s_z")
        s_gnn = sem("s_gnn")
        s_x1 = sem("s_x1")
        s_hi2 = sem("s_hi2")
        s_lo2 = sem("s_lo2")
        s_gT = [sem(f"s_gT{j}") for j in range(GROUP)]
        s_sp = sem("s_sp")
        s_score = sem("s_score")
        s_route = sem("s_route")
        s_chose = sem("s_chose")
        s_pp = sem("s_pp")
        s_step = sem("s_step")
        s_place = sem("s_place")
        s_scat = [sem(f"s_scat{j}") for j in range(RING // GROUP)]
        s_free = sem("s_free")
        s_w = [sem(f"s_w{k}") for k in range(WRING)]
        s_wsc = sem("s_wsc")
        s_wh = sem("s_wh")
        s_wl = sem("s_wl")
        s_zeros = sem("s_zeros")
        s_cntp = sem("s_cntp")
        s_tab = sem("s_tab")
        s_tables = sem("s_tables")
        s_pad = sem("s_pad")
        s_listed = sem("s_listed")
        s_xT = [sem(f"s_xT{k}") for k in range(2)]
        s_dest = [sem(f"s_dest{k}") for k in range(2)]
        s_hp = sem("s_hp")
        s_gelu = sem("s_gelu")
        s_hh = sem("s_hh")
        s_hl = sem("s_hl")
        s_yp = sem("s_yp")
        s_y = sem("s_y")
        s_part = [sem(f"s_part{k}") for k in range(2)]
        s_ge = sem("s_ge")
        s_gate = sem("s_gate")
        s_pt = [sem(f"s_pt{k}") for k in range(CR)]
        s_sum0 = sem("s_sum0")
        s_sum = sem("s_sum")
        s_out = sem("s_out")
        s_apart = sem("s_apart")

        x_dram = x.rearrange("b k d -> (b k) d").rearrange("(t p) d -> p t d", p=P)
        out_dram = out.rearrange("b k d -> (b k) d").rearrange("(t p) d -> p t d", p=P)
        X3 = X[:, :].rearrange("p (t d) -> p t d", d=D)

        N_CONST = 11

        def in_loop(s):
            return not isinstance(s, int)

        def has(s, g):
            return in_loop(s) or 0 <= g < GROUPS

        def has_tile(s, t):
            return in_loop(s) or 0 <= t < TILES

        def wait(eng, semaphore, value):
            if not isinstance(value, int) or value > 0:
                eng.wait_ge(semaphore, value)

        def apart(eng, s):
            if in_loop(s):
                eng.sem_inc(s_apart, 1)

        def ring(g):
            return (g % (RING // GROUP)) * GROUP

        block = ctx.enter_context(nc.Block())

        @block.sync
        def _(sp):
            sp.dma_start(X3[:, 0:GROUP, :], x_dram[:, 0:GROUP, :]).then_inc(s_x, 16)
            sp.wait_ge(s_adjz, 1)
            sp.dma_start(adjt_i[0:NODES, 0:NODES], adj_t).then_inc(s_adj, 16)
            sp.dma_start(adjt_i[NODES:P, NODES:P], adj_t).then_inc(s_adj, 16)
            sp.dma_start(adj_i[0:NODES, :], adj).then_inc(s_adj, 16)
            sp.dma_start(adj_i[NODES:P, :], adj).then_inc(s_adj, 16)
            w1_dram = w1.rearrange("x (c p) h -> p x c h", p=P)
            w2_dram = w2.rearrange("x (c p) h -> p x c h", p=P)

            def w_load(k):
                e, which = k % EXPERTS, k // EXPERTS
                src = (w1_dram, w2_dram)[which][:, e]
                a = (k % WRING) * WCOLS
                wait(sp, s_wl, k - WRING + 1)
                sp.dma_start(w_in[:, a:a + WCOLS].rearrange("p (c h) -> p c h", h=src.shape[2]),
                             src).then_inc(s_w[k % WRING], 16)

            for k in range(2 * EXPERTS):
                g = k + 1
                if g < AHEAD:
                    sp.wait_ge(s_x, 16 * g)
                    sp.dma_start(X3[:, g * GROUP:(g + 1) * GROUP, :],
                                 x_dram[:, g * GROUP:(g + 1) * GROUP, :]).then_inc(s_x, 16)
                w_load(k)

            def transposes(g):
                for j in range(GROUP):
                    t = g * GROUP + j
                    sp.wait_ge(s_lo2, t + 1)
                    apart(sp, g)
                    wait(sp, s_sp, t - GROUP + 1)
                    apart(sp, g)
                    sp.dma_start_transpose(
                        gT[:, j * 2 * D:(j + 1) * 2 * D].rearrange("p (c t) -> p c t", t=P),
                        row16[:, ds((ring(g) + j) * ROW16, 2 * D)]).then_inc(s_gT[j], 16)

            def load_and_transpose(g):
                sp.wait_ge(s_x, (g + AHEAD) * 16)
                sp.dma_start(X3[:, ds((g + AHEAD) * GROUP, GROUP), :],
                             x_dram[:, ds((g + AHEAD) * GROUP, GROUP), :]).then_inc(s_x, 16)
                transposes(g)

            load_and_transpose(0)
            with sp.Fori(1, GROUPS - AHEAD) as g:
                load_and_transpose(g)
            with sp.Fori(GROUPS - AHEAD, GROUPS) as g:
                transposes(g)

            sp.wait_ge(s_zeros, 1)
            sp.wait_ge(s_tables, 1)
            for e in range(EXPERTS):
                r = sp.value_load(list_end[0:1, e:e + 1], min_val=0, max_val=ROWS - BLOCK)
                sp.dma_start(lists[ds(r, BLOCK), :].rearrange("(p h) c -> p (h c)", h=HALVES),
                             zeros[:, :]).then_inc(s_pad, 16)
            sp.dma_start(lists[ZERO_LIST:ROWS, :].rearrange("(p h) c -> p (h c)", h=HALVES),
                         zeros[:, :]).then_inc(s_pad, 16)
            sp.wait_ge(s_pad, 16 * (EXPERTS + 1))
            sp.wait_ge(s_listed, 1)
            sp.wait_ge(s_tables, 2)

            def load_rows(b, k):
                r = sp.value_load(start[0:1, ds(b, 1)], min_val=0, max_val=ROWS - BLOCK)
                wait(sp, s_hp, HC * (b - 1))
                sp.dma_start_transpose(
                    xT[:, k * 2 * DC * BLOCK:(k + 1) * 2 * DC * BLOCK]
                    .rearrange("p (c t) -> p c t", t=BLOCK),
                    lists16[ds(r, BLOCK), 0:2 * D]).then_inc(s_xT[k], 16)

            def load_dest(b, k, n):
                r = sp.value_load(start[0:1, ds(b, 1)], min_val=0, max_val=ROWS - BLOCK)
                e = sp.value_load(owner[0:1, ds(b, 1)], min_val=0, max_val=EXPERTS - 1)
                wait(sp, s_part[k], 16 * HALVES * n)
                sp.dma_start(dest[:, k * HALVES:(k + 1) * HALVES],
                             lists[ds(r, BLOCK), ds(e + D, 1)].rearrange("(h p) c -> p (h c)", p=P),
                             allow_slow_non_contiguous=True).then_inc(s_dest[k], 16)

            load_rows(0, 0)
            load_rows(1, 1)
            load_rows(2, 0)
            load_dest(0, 0, 0)
            load_rows(3, 1)
            load_dest(1, 1, 0)
            with sp.Fori(2, BLOCKS // 2) as n:
                load_rows(2 * n, 0)
                load_dest(2 * n - 2, 0, n - 1)
                load_rows(2 * n + 1, 1)
                load_dest(2 * n - 1, 1, n - 1)
            load_dest(BLOCKS - 2, 0, BLOCKS // 2 - 1)
            load_dest(BLOCKS - 1, 1, BLOCKS // 2 - 1)

            for k in range(2):
                sp.wait_ge(s_part[k], 16 * HALVES * (BLOCKS // 2))
            ranks = parts.rearrange("(r t p) d -> p r t d", p=P, r=2)

            def part_load(g, k):
                wait(sp, s_sum, (g - CR + 1) * GROUP)
                a = k * 2 * GROUP * D
                for r in range(2):
                    sp.dma_start(pt[:, a + r * GROUP * D:a + (r + 1) * GROUP * D]
                                 .rearrange("p (t d) -> p t d", d=D),
                                 ranks[:, r, ds(g * GROUP, GROUP), :]).then_inc(s_pt[k], 16)

            for k in range(CR):
                part_load(k, k)
            with sp.Fori(1, GROUPS // CR) as n:
                for k in range(CR):
                    part_load(n * CR + k, k)

        @block.gpsimd
        def _(pool):
            nc.gpsimd.memset(adjt_i[:, :], 0).then_inc(s_adjz, 1)
            z3 = zeros[:, :].rearrange("p (h c) -> p h c", c=ROW32)
            nc.gpsimd.memset(z3[:, :, 0:D], 0)
            nc.gpsimd.memset(z3[:, :, D:ROW32], NOWHERE).then_inc(s_zeros, 1)

            pool.wait_ge(s_const, 16 * N_CONST)
            m = const("mask")
            nc.gpsimd.tensor_copy(bpart[:, 0:D], bb[:, :]).then_inc(s_bias, 1)
            pool.wait_ge(s_bias, 1)
            nc.gpsimd.tensor_tensor(brest[:, 0:D], bb[:, :], bpart[:, 0:D], ALU.subtract).then_inc(s_bias, 1)
            pool.wait_ge(s_bias, 2)
            nc.gpsimd.tensor_copy(bpart[:, D:2 * D], brest[:, 0:D]).then_inc(s_bias, 1)
            pool.wait_ge(s_bias, 3)
            nc.gpsimd.tensor_tensor(brest[:, D:2 * D], brest[:, 0:D], bpart[:, D:2 * D],
                                    ALU.subtract).then_inc(s_bias, 1)
            pool.wait_ge(s_bias, 4)
            nc.gpsimd.tensor_copy(bpart[:, 2 * D:3 * D], brest[:, D:2 * D]).then_inc(s_bias, 1)
            pool.wait_ge(s_bias, 5)
            nc.gpsimd.tensor_scalar(bmask[:, 0:D], bpart[:, 0:D], m[:, 0:1], 1.0, ALU.mult, ALU.mult)
            nc.gpsimd.tensor_scalar(bmask[:, D:2 * D], bpart[:, D:2 * D], m[:, 1:2], 1.0,
                                    ALU.mult, ALU.mult).then_inc(s_bias, 1)
            pool.wait_ge(s_bias, 6)
            nc.gpsimd.tensor_tensor(bmask[:, 0:D], bmask[:, 0:D], bmask[:, D:2 * D], ALU.add).then_inc(s_bias, 1)
            pool.wait_ge(s_bias, 7)
            nc.gpsimd.tensor_scalar(bmask[:, D:2 * D], bpart[:, 2 * D:3 * D], m[:, 2:3], 1.0,
                                    ALU.mult, ALU.mult).then_inc(s_bias, 1)
            pool.wait_ge(s_bias, 8)
            nc.gpsimd.tensor_tensor(bias_rows[:, :], bmask[:, 0:D], bmask[:, D:2 * D], ALU.add).then_inc(s_bias, 1)

            for k in range(2 * EXPERTS):
                e, which = k % EXPERTS, k // EXPERTS
                a = (k % WRING) * WCOLS
                hi = (w1h, w2h)[which][:, e * WCOLS:(e + 1) * WCOLS]
                lo = (w1l, w2l)[which][:, e * WCOLS:(e + 1) * WCOLS]
                pool.wait_ge(s_w[k % WRING], 16 * (k // WRING + 1))
                wait(pool, s_wl, k)
                nc.gpsimd.tensor_scalar(w_sc[:, :], w_in[:, a:a + WCOLS], W_SCALE, 1.0,
                                        ALU.mult, ALU.mult).then_inc(s_wsc, 1)
                pool.wait_ge(s_wsc, k + 1)
                pool.wait_ge(s_wh, k + 1)
                nc.gpsimd.tensor_tensor(lo, w_sc[:, :], hi, ALU.subtract).then_inc(s_wl, 1)

            def scatters(g, k):
                pool.wait_ge(s_place, g + 1)
                apart(pool, g)
                for j in range(GROUP):
                    slot = k * GROUP + j
                    for r in range(2):
                        pool.indirect_dma_start(
                            out=lists,
                            out_offset=bass.IndirectOffsetOnAxis(
                                ap=place[:, 2 * slot + r:2 * slot + r + 1], axis=0),
                            in_=row[:, slot * ROW32:(slot + 1) * ROW32], in_offset=None,
                        ).then_inc(s_scat[k], 16)

            NR = RING // GROUP
            PER = 16 * 2 * GROUP

            def scattered(n, k):
                pool.wait_ge(s_scat[k], PER * (n + 1))
                pool.sem_inc(s_free, 1)

            scatters(0, 0)
            for k in range(1, NR):
                scattered(0, k - 1)
                scatters(k, k)
            with pool.Fori(1, GROUPS // NR) as n:
                scattered(n - 1, NR - 1)
                scatters(n * NR, 0)
                for k in range(1, NR):
                    scattered(n, k - 1)
                    scatters(n * NR + k, k)
            pool.wait_ge(s_scat[NR - 1], PER * (GROUPS // NR))
            pool.sem_inc(s_listed, 1)

            def part_scatter(b, k, n):
                pool.wait_ge(s_dest[k], 16 * (n + 1))
                pool.wait_ge(s_y, b + 1)
                apart(pool, b)
                for h in range(HALVES):
                    i = k * HALVES + h
                    pool.indirect_dma_start(
                        out=parts,
                        out_offset=bass.IndirectOffsetOnAxis(ap=dest[:, i:i + 1], axis=0),
                        in_=y[:, i * D:(i + 1) * D], in_offset=None,
                        bounds_check=2 * TOKENS - 1, oob_is_err=False,
                    ).then_inc(s_part[k], 16)

            with pool.Fori(0, BLOCKS // 2) as n:
                part_scatter(2 * n, 0, n)
                part_scatter(2 * n + 1, 1, n)

        @block.scalar
        def _(act):
            act.dma_start(cf[:, :], consts_f).then_inc(s_const, 16)
            act.dma_start(ch[:, :], consts_h).then_inc(s_const, 16)
            act.dma_start(gw[:, :].rearrange("p (c o) -> p c o", o=D),
                          gnn_wt.rearrange("(c p) o -> p c o", p=P)).then_inc(s_const, 16)
            act.dma_start(bb[:, :], gnn_b.partition_broadcast(P)).then_inc(s_const, 16)
            act.dma_start(wg_f[:, :].rearrange("p (c e) -> p c e", e=EXPERTS),
                          wg.rearrange("(c p) e -> p c e", p=P)).then_inc(s_const, 16)
            act.dma_start(b1s[:, :], b1_t).then_inc(s_const, 16)
            act.dma_start(b2s[:, :], b2.rearrange("x e -> (x e)").partition_broadcast(P)).then_inc(s_const, 16)
            for j in range(GROUP - 1):
                act.dma_start(bg4[:, j * EXPERTS:(j + 1) * EXPERTS], bg.partition_broadcast(P)).then_inc(s_const, 16)
            act.dma_start(bg4[:, (GROUP - 1) * EXPERTS:], bg.partition_broadcast(P)).then_inc(s_const, 16)
            act.wait_ge(s_const, 16 * N_CONST)

            def step(s, j):
                tau = GROUP * s + j
                if has_tile(s, tau):
                    k = j
                    src = X[:, ds(tau * D, D)]
                    act.wait_ge(s_nm1, s + 1)
                    wait(act, s_lo1, tau - 3)
                    wait(act, s_nbp, tau - 3)
                    nc.scalar.activation(xf1[:, k * D:(k + 1) * D], src, ACT.Identity,
                                         bias=nm1[:, ds(tau, 1)], scale=rs1[:, ds(tau, 1)])
                    nc.scalar.activation(xn1[:, k * 2 * D:k * 2 * D + D], src, ACT.Identity,
                                         bias=nm1[:, ds(tau, 1)], scale=rs1[:, ds(tau, 1)]).then_inc(s_hi1, 1)
                if has_tile(s, tau - 3):
                    k = (j + 1) % 2
                    act.wait_ge(s_nbp, tau - 2)
                    wait(act, s_gnn, tau - 4)
                    nc.scalar.activation(z[:, k * 2 * D:(k + 1) * 2 * D], ps_nb[k][:, :], ACT.Copy,
                                         scale=1.0 / X_SCALE).then_inc(s_z, 1)
                if has_tile(s, tau - 11):
                    t = tau - 11
                    g, jj = (s - 2, 0) if j == 3 else (s - 3, j + 1)
                    k = (j + 1) % 2
                    src = X[:, ds(t * D, D)]
                    act.wait_ge(s_nm2, g + 1)
                    wait(act, s_lo2, t - 1)
                    wait(act, s_free, g - RING // GROUP + 1)
                    nc.scalar.activation(xf2[:, k * D:(k + 1) * D], src, ACT.Identity,
                                         bias=nm2[:, ds(t, 1)], scale=rs2[:, ds(t, 1)])
                    nc.scalar.activation(row16[:, ds((ring(g) + jj) * ROW16, D)], src, ACT.Identity,
                                         bias=nm2[:, ds(t, 1)], scale=rs2[:, ds(t, 1)]).then_inc(s_hi2, 1)
                if j == 2 and has(s, s + 1):
                    g = s + 1
                    act.wait_ge(s_mvc1, g + 1)
                    nc.scalar.activation(sd1[:, :], mvc1[:, 1:2 * GROUP:2], ACT.Sqrt,
                                         bias=const("eps"), scale=1.0 / X_SCALE ** 2).then_inc(s_sd1, 1)
                if j == 1 and has(s, s - 2):
                    g = s - 2
                    act.wait_ge(s_mvc2, g + 1)
                    nc.scalar.activation(sd2[:, :], mvc2[:, 1:2 * GROUP:2], ACT.Sqrt,
                                         bias=const("eps"), scale=1.0 / X_SCALE ** 2).then_inc(s_sd2, 1)

            for s in range(-1, 7):
                for j in range(GROUP):
                    step(s, j)
            with act.Fori(7, GROUPS - 1) as s:
                for j in range(GROUP):
                    step(s, j)
            for s in range(GROUPS - 1, GROUPS + 3):
                for j in range(GROUP):
                    step(s, j)

            def gelus(b, k):
                e = act.value_load(owner[0:1, ds(b, 1)], min_val=0, max_val=EXPERTS - 1)
                for c in range(HC):
                    act.wait_ge(s_hp, HC * b + c + 1)
                    wait(act, s_hl, HC * (b - 2) + c + 1)
                    a = (k * HC + c) * BLOCK
                    nc.scalar.activation(hf[:, a:a + BLOCK], ps_h[k][c][:, 0:BLOCK], ACT.Gelu,
                                         bias=b1s[:, ds(e * HC + c, 1)],
                                         scale=1.0 / (X_SCALE * W_SCALE)).then_inc(s_gelu, 1)

            act.wait_ge(s_tables, 2)
            gelus(0, 0)
            gelus(1, 1)
            with act.Fori(1, BLOCKS // 2) as n:
                gelus(2 * n, 0)
                gelus(2 * n + 1, 1)
            nc.scalar.activation(ge[:, :], gap[:, :], ACT.Exp).then_inc(s_ge, 1)

            with act.Fori(0, GROUPS) as g:
                act.wait_ge(s_sum, GROUP * (g + 1))
                act.dma_start(out_dram[:, ds(g * GROUP, GROUP), :],
                              X3[:, ds(g * GROUP, GROUP), :]).then_inc(s_out, 16)
            act.wait_ge(s_out, 16 * GROUPS)

        @block.tensor
        def _(pe):
            mm = nc.tensor.matmul
            pe.wait_ge(s_const, 16 * N_CONST)
            pe.wait_ge(s_nb, 1)
            mm(ps_place[:, 0:P], ones, nb[:, 0:P], start=True, stop=True).then_inc(s_degp, 1)
            pe.wait_ge(s_deg, 1)
            pe.wait_ge(s_nb, 2)
            pe.wait_ge(s_bias, 9)
            pe.wait_ge(s_wgr, 1)

            def step(s, j):
                tau = GROUP * s + j
                if has_tile(s, tau - 2):
                    k, slot = j % 2, (j + 2) % 4
                    pe.wait_ge(s_lo1, tau - 1)
                    wait(pe, s_z, tau - 3)
                    for c in range(DC):
                        for part in range(2):
                            a = slot * 2 * D + part * D + c * P
                            last = mm(ps_nb[k][:, c * 2 * P:(c + 1) * 2 * P], xn1[:, a:a + P], nb[:, :],
                                      start=part == 0, stop=part == 1)
                    last.then_inc(s_nbp, 1)
                if has_tile(s, tau - 4):
                    k = j % 2
                    o = ps_gnn[k][:, 0:D]
                    pe.wait_ge(s_z, tau - 3)
                    wait(pe, s_x1, tau - 5)
                    mm(o, deg_rows[:, :], bias_rows[:, :], start=True, stop=False)
                    for c in range(DC):
                        a = k * 2 * D + c * 2 * P
                        mm(o, z[:, a:a + P], gw[:, (DC + c) * D:(DC + c + 1) * D], start=False, stop=False)
                        last = mm(o, z[:, a + P:a + 2 * P], gw[:, c * D:(c + 1) * D],
                                  start=False, stop=c == DC - 1)
                    last.then_inc(s_gnn, 1)
                if j == 0 and has(s, s - 5):
                    g = s - 5
                    pe.wait_ge(s_chose, g + 1)
                    n = EXPERTS
                    mm(ps_place[:, 0:GROUP * n], below, chose[:, :], start=True, stop=False)
                    for i in range(GROUP):
                        mm(ps_place[:, i * n:(i + 1) * n], ones, before[:, :], start=False, stop=False)
                        for q in range(i):
                            last = mm(ps_place[:, i * n:(i + 1) * n], ones, chose[:, q * n:(q + 1) * n],
                                      start=False, stop=(i, q) == (GROUP - 1, GROUP - 2))
                    last.then_inc(s_pp, 1)
                if has_tile(s, tau - 14):
                    g, jj = (s - 4, j + 2) if j < 2 else (s - 3, j - 2)
                    pe.wait_ge(s_gT[jj], 16 * (g + 1))
                    wait(pe, s_score, g)
                    o = ps_score[:, jj * EXPERTS:(jj + 1) * EXPERTS]
                    for c in range(DC):
                        hi = gT[:, jj * 2 * D + c * P:jj * 2 * D + (c + 1) * P]
                        lo = gT[:, jj * 2 * D + D + c * P:jj * 2 * D + D + (c + 1) * P]
                        wh = wg_h[:, c * EXPERTS:(c + 1) * EXPERTS]
                        wl = wg_h[:, (DC + c) * EXPERTS:(DC + c + 1) * EXPERTS]
                        mm(o, hi, wl, start=c == 0, stop=False)
                        mm(o, lo, wh, start=False, stop=False)
                        last = mm(o, hi, wh, start=False, stop=c == DC - 1)
                    last.then_inc(s_sp, 1)

            for s in range(0, 5):
                for j in range(GROUP):
                    step(s, j)
            with pe.Fori(5, GROUPS) as s:
                for j in range(GROUP):
                    step(s, j)
            for s in range(GROUPS, GROUPS + 6):
                for j in range(GROUP):
                    step(s, j)
            pe.wait_ge(s_place, GROUPS)
            mm(ps_place[:, 0:EXPERTS], ones, before[:, :], start=True, stop=True).then_inc(s_cntp, 1)

            w_at = [pe.alloc_register(f"w_at{k}") for k in range(2)]

            def owner_weights(b, k):
                pe.reg_load(w_at[k], weights_at[0:1, ds(b, 1)])

            def base(k):
                return pe.snap(w_at[k], donate=False, min_val=0, max_val=(EXPERTS - 1) * WCOLS)

            def hidden(b, k, n):
                owner_weights(b, k)
                w0 = base(k)
                pe.wait_ge(s_xT[k], 16 * (n + 1))
                wait(pe, s_gelu, HC * (b - 1))
                for h in range(HC):
                    o = ps_h[k][h][:, 0:BLOCK]
                    for c in range(DC):
                        a = k * 2 * DC * BLOCK + c * BLOCK
                        hi, lo = xT[:, a:a + BLOCK], xT[:, a + DC * BLOCK:a + (DC + 1) * BLOCK]
                        w = ds(w0 + (c * H + h * P), P)
                        mm(o, w1l[:, w], hi, start=c == 0, stop=False)
                        mm(o, w1h[:, w], lo, start=False, stop=False)
                        last = mm(o, w1h[:, w], hi, start=False, stop=c == DC - 1)
                    last.then_inc(s_hp, 1)

            def output(b, k):
                w0 = base(k)
                wait(pe, s_y, b - 1)
                for h in range(HC):
                    pe.wait_ge(s_hl, HC * b + h + 1)
                    w = ds(w0 + h * D, D)
                    for left, right in ((hl, w2h), (hh, w2h), (hh, w2l)):
                        for m in range(HALVES):
                            a = (k * HC + h) * BLOCK + m * P
                            last = mm(ps_y[k][:, m * D:(m + 1) * D], left[:, a:a + P], right[:, w],
                                      start=(h, m) == (0, 0) and left is hl,
                                      stop=(h, m) == (HC - 1, 1) and right is w2l,
                                      skip_group_check=True)
                last.then_inc(s_yp, 1)

            pe.wait_ge(s_tables, 2)
            pe.wait_ge(s_wl, 2 * EXPERTS)
            hidden(0, 0, 0)
            hidden(1, 1, 0)
            output(0, 0)
            hidden(2, 0, 1)
            output(1, 1)
            hidden(3, 1, 1)
            output(2, 0)
            with pe.Fori(2, BLOCKS // 2) as n:
                hidden(2 * n, 0, n)
                output(2 * n - 1, 1)
                hidden(2 * n + 1, 1, n)
                output(2 * n, 0)
            output(BLOCKS - 1, 1)

        @block.vector
        def _(dve):
            v = nc.vector
            dve.wait_ge(s_const, 16 * N_CONST)
            dve.wait_ge(s_adj, 64)
            v.tensor_copy(nb[:, 0:P], adjt_i[:, :]).then_inc(s_nb, 1)
            v.tensor_copy(adj_f[:, :], adj_i[:, :]).then_inc(s_setup, 1)
            v.tensor_scalar(wg_s[:, :], wg_f[:, :], W_SCALE, None, ALU.mult).then_inc(s_setup, 1)
            v.memset(before[:, :], 0.0)
            dve.wait_ge(s_setup, 1)
            v.tensor_reduce(deg[:, :], adj_f[:, :], AX_X, ALU.add).then_inc(s_setup, 1)
            NW = DC * EXPERTS
            dve.wait_ge(s_setup, 2)
            v.tensor_copy(wg_h[:, 0:NW], wg_s[:, :]).then_inc(s_setup, 1)
            dve.wait_ge(s_setup, 3)
            v.tensor_scalar(nb[:, P:2 * P], const("ident"), deg[:, 0:1], None, ALU.mult).then_inc(s_nb, 1)
            dve.wait_ge(s_setup, 4)
            v.tensor_tensor(wg_h[:, NW:2 * NW], wg_s[:, :], wg_h[:, 0:NW], ALU.subtract).then_inc(s_wgr, 1)
            dve.wait_ge(s_degp, 1)
            v.tensor_scalar(deg_rows[:, :], ps_place[:, 0:P], const("mask3"), None, ALU.mult).then_inc(s_deg, 1)

            def cut_weights(k):
                e, which = k % EXPERTS, k // EXPERTS
                a = (k % WRING) * WCOLS
                dve.wait_ge(s_w[k % WRING], 16 * (k // WRING + 1))
                v.tensor_scalar((w1h, w2h)[which][:, e * WCOLS:(e + 1) * WCOLS], w_in[:, a:a + WCOLS],
                                W_SCALE, None, ALU.mult).then_inc(s_wh, 1)

            def step(s, j):
                tau = GROUP * s + j
                if j == 2 and has(s, s - 4):
                    g = s - 4
                    dve.wait_ge(s_sp, GROUP * (g + 1))
                    v.scalar_tensor_tensor(
                        out=score[:, :], in0=ps_score[:, 0:GROUP * EXPERTS],
                        scalar=1.0 / (X_SCALE * W_SCALE), in1=bg4[:, :],
                        op0=ALU.mult, op1=ALU.add).then_inc(s_score, 1)
                if has_tile(s, tau - 1):
                    k = (j + 3) % 4
                    dve.wait_ge(s_hi1, tau)
                    v.tensor_tensor(xn1[:, k * 2 * D + D:(k + 1) * 2 * D], xf1[:, k * D:(k + 1) * D],
                                    xn1[:, k * 2 * D:k * 2 * D + D], ALU.subtract).then_inc(s_lo1, 1)
                if has_tile(s, tau - 5):
                    k = (j + 1) % 2
                    xt = X[:, ds((tau - 5) * D, D)]
                    dve.wait_ge(s_gnn, tau - 4)
                    v.tensor_tensor(xt, ps_gnn[k][:, 0:D], xt, ALU.add).then_inc(s_x1, 1)
                if j == 3 and has(s, s + 1):
                    g = s + 1
                    dve.wait_ge(s_sd1, g + 1)
                    v.reciprocal(rs1[:, ds(g * GROUP, GROUP)], sd1[:, :]).then_inc(s_rs1, 1)
                if j == 2 and has(s, s - 2):
                    g = s - 2
                    dve.wait_ge(s_sd2, g + 1)
                    v.reciprocal(rs2[:, ds(g * GROUP, GROUP)], sd2[:, :]).then_inc(s_rs2, 1)
                if has_tile(s, tau + 6):
                    g, jj = (s + 2, j - 2) if j > 1 else (s + 1, j + 2)
                    if jj == 0 or not in_loop(s):
                        dve.wait_ge(s_x, 16 * (g + 1))
                    v.bn_stats(stat1[:, (jj % 2) * 6:(jj % 2) * 6 + 6],
                               X[:, ds((tau + 6) * D, D)]).then_inc(s_bn1, 1)
                if j == 3 and has(s, s + 1):
                    g = s + 1
                    dve.wait_ge(s_rs1, g + 1)
                    v.scalar_tensor_tensor(
                        out=nm1[:, ds(g * GROUP, GROUP)], in0=mvc1[:, 0:2 * GROUP:2], scalar=-1.0,
                        in1=rs1[:, ds(g * GROUP, GROUP)], op0=ALU.mult, op1=ALU.mult).then_inc(s_nm1, 1)
                if has_tile(s, tau - 5):
                    jj = (j + 3) % 4
                    dve.wait_ge(s_x1, tau - 4)
                    apart(dve, s)
                    v.bn_stats(stat2[:, (jj % 2) * 6:(jj % 2) * 6 + 6],
                               X[:, ds((tau - 5) * D, D)]).then_inc(s_bn2, 1)
                if j == 2 and has(s, s - 2):
                    g = s - 2
                    dve.wait_ge(s_rs2, g + 1)
                    v.scalar_tensor_tensor(
                        out=nm2[:, ds(g * GROUP, GROUP)], in0=mvc2[:, 0:2 * GROUP:2], scalar=-1.0,
                        in1=rs2[:, ds(g * GROUP, GROUP)], op0=ALU.mult, op1=ALU.mult).then_inc(s_nm2, 1)
                if has_tile(s, tau - 12):
                    g, k = s - 3, j % 2
                    a = (ring(g) + j) * ROW16
                    dve.wait_ge(s_hi2, tau - 11)
                    v.tensor_tensor(row16[:, ds(a + D, D)], xf2[:, k * D:(k + 1) * D],
                                    row16[:, ds(a, D)], ALU.subtract).then_inc(s_lo2, 1)
                if has_tile(s, tau + 6):
                    jj = (j + 2) % 4
                    if j == 2:
                        wait(dve, s_mvc1, s + 2)
                    dve.wait_ge(s_bn1, tau + 7)
                    apart(dve, s)
                    v.bn_aggr(mv1[:, 2 * jj:2 * jj + 2], stat1[:, (jj % 2) * 6:(jj % 2) * 6 + 6]).then_inc(s_mv1, 1)
                if has_tile(s, tau - 5):
                    jj = (j + 3) % 4
                    if j == 1:
                        wait(dve, s_mvc2, s - 1)
                    dve.wait_ge(s_bn2, tau - 4)
                    apart(dve, s)
                    v.bn_aggr(mv2[:, 2 * jj:2 * jj + 2], stat2[:, (jj % 2) * 6:(jj % 2) * 6 + 6]).then_inc(s_mv2, 1)
                if j == 2 and has(s, s - 4):
                    choose(s - 4)
                if j == 1 and has(s, s - 5):
                    find_places(s - 5)
                if j == 1 and has(s, s + 1):
                    g = s + 1
                    wait(dve, s_nm1, g)
                    dve.wait_ge(s_mv1, GROUP * (g + 1))
                    v.tensor_copy(mvc1[:, :], mv1[:, :]).then_inc(s_mvc1, 1)
                if j == 0 and has(s, s - 2):
                    g = s - 2
                    wait(dve, s_nm2, g)
                    dve.wait_ge(s_mv2, GROUP * (g + 1))
                    v.tensor_copy(mvc2[:, :], mv2[:, :]).then_inc(s_mvc2, 1)

            def choose(g):
                n = EXPERTS
                dve.wait_ge(s_score, g + 1)
                apart(dve, g)
                for i in range(GROUP):
                    last = v.max(best[:, 8 * i:8 * i + 8], score[:, n * i:n * (i + 1)])
                last.then_inc(s_route, 1)
                dve.wait_ge(s_route, 5 * g + 1)
                apart(dve, g)
                for i in range(GROUP):
                    last = v.max_index(best_i[:, 8 * i:8 * i + 8], best[:, 8 * i:8 * i + 8],
                                       score[:, n * i:n * (i + 1)])
                last.then_inc(s_route, 1)
                b3 = best[:, :].rearrange("p (t k) -> p t k", k=8)
                v.tensor_tensor(gap[:, ds(g * GROUP, GROUP)], b3[:, :, 1], b3[:, :, 0], ALU.subtract)
                dve.wait_ge(s_route, 5 * g + 2)
                v.tensor_copy(best_f[:, :].rearrange("p (t r) -> p t r", r=2),
                              best_i[:, :].rearrange("p (t k) -> p t k", k=8)[:, :, 0:2]).then_inc(s_route, 1)
                dve.wait_ge(s_route, 5 * g + 3)
                v.tensor_tensor(chose2[:, :].rearrange("p (q e) -> p q e", e=n),
                                const("iota").rearrange("p (q e) -> p q e", e=n),
                                best_f[:, :].unsqueeze(2).to_broadcast([P, 2 * GROUP, n]),
                                ALU.is_equal).then_inc(s_route, 1)
                dve.wait_ge(s_route, 5 * g + 4)
                c4 = chose2[:, :].rearrange("p (t r e) -> p t r e", r=2, e=n)
                v.tensor_tensor(chose[:, :].rearrange("p (t e) -> p t e", e=n),
                                c4[:, :, 0, :], c4[:, :, 1, :], ALU.add).then_inc(s_chose, 1)
                v.scalar_tensor_tensor(
                    out=row[:, ds(ring(g) * ROW32, GROUP * ROW32)]
                    .rearrange("p (t c) -> p t c", c=ROW32)[:, :, D:ROW32],
                    in0=c4[:, :, 1, :], scalar=float(TOKENS),
                    in1=const_token(g).unsqueeze(2).to_broadcast([P, GROUP, n]),
                    op0=ALU.mult, op1=ALU.add)
                dve.wait_ge(s_chose, g + 1)
                v.tensor_reduce(chose_g[:, :], chose[:, :].rearrange("p (t e) -> p e t", e=n),
                                AX_X, ALU.add).then_inc(s_route, 1)

            def const_token(g):
                a, _ = cols["token"]
                return cf[:, ds(g * GROUP + a, GROUP)]

            def find_places(g):
                n = EXPERTS
                dve.wait_ge(s_pp, g + 1)
                v.tensor_tensor(place_e[:, :], ps_place[:, 0:GROUP * n], const("list_start"),
                                ALU.add).then_inc(s_step, 1)
                dve.wait_ge(s_route, 5 * g + 5)
                v.tensor_tensor(before[:, :], before[:, :], chose_g[:, :], ALU.add)
                dve.wait_ge(s_step, 3 * g + 1)
                v.tensor_tensor(place2[:, :].rearrange("p (t r e) -> p t r e", r=2, e=n),
                                chose2[:, :].rearrange("p (t r e) -> p t r e", r=2, e=n),
                                place_e[:, :].rearrange("p (t e) -> p t e", e=n).unsqueeze(2)
                                .to_broadcast([P, GROUP, 2, n]), ALU.mult).then_inc(s_step, 1)
                dve.wait_ge(s_step, 3 * g + 2)
                v.tensor_reduce(place_f[:, :], place2[:, :].rearrange("p (q e) -> p q e", e=n), AX_X,
                                ALU.add).then_inc(s_step, 1)
                dve.wait_ge(s_step, 3 * g + 3)
                v.tensor_copy(place[:, ds(2 * ring(g), 2 * GROUP)], place_f[:, :]).then_inc(s_place, 1)

            k = 0
            for s in range(-2, 5):
                for j in range(GROUP):
                    step(s, j)
                    if s >= -1 and k < 2 * EXPERTS:
                        cut_weights(k)
                        k += 1
            with dve.Fori(5, GROUPS - 2) as s:
                for j in range(GROUP):
                    step(s, j)
            for s in range(GROUPS - 2, GROUPS + 5):
                for j in range(GROUP):
                    step(s, j)

            n, most = EXPERTS, TOKENS // BLOCK
            dve.wait_ge(s_cntp, 1)
            v.tensor_copy(count[:, :], ps_place[:, 0:n]).then_inc(s_tab, 1)
            dve.wait_ge(s_tab, 1)
            v.tensor_tensor(list_end[:, :], count[:, :], const("list_start")[:, 0:n], ALU.add).then_inc(s_tables, 1)
            v.tensor_tensor(full[:, :].rearrange("p (e k) -> p e k", k=most),
                            count[:, :].unsqueeze(2).to_broadcast([P, n, most]),
                            const("whole").rearrange("p (e k) -> p e k", k=most), ALU.is_gt).then_inc(s_tab, 1)
            dve.wait_ge(s_tab, 2)
            v.tensor_reduce(nblk[:, :], full[:, :].rearrange("p (e k) -> p e k", k=most), AX_X,
                            ALU.add).then_inc(s_tab, 1)
            dve.wait_ge(s_tab, 3)
            v.tensor_tensor_scan(cum[:, :], nblk[:, :], const("zero"), 0.0, ALU.add, ALU.add).then_inc(s_tab, 1)
            v.tensor_scalar(skip[:, :], nblk[:, :], -float(BLOCK), float(LIST_ROWS), ALU.mult,
                            ALU.add).then_inc(s_tab, 1)
            dve.wait_ge(s_tab, 5)
            p3 = passed[:, :].rearrange("p (b e) -> p b e", e=n)
            v.tensor_tensor(p3, cum[:, :].unsqueeze(1).to_broadcast([P, BLOCKS, n]),
                            const("block").unsqueeze(2).to_broadcast([P, BLOCKS, n]),
                            ALU.is_le).then_inc(s_tab, 1)
            dve.wait_ge(s_tab, 6)
            v.tensor_tensor(skipped[:, :].rearrange("p (b e) -> p b e", e=n), p3,
                            skip[:, :].unsqueeze(1).to_broadcast([P, BLOCKS, n]), ALU.mult).then_inc(s_tab, 1)
            v.tensor_reduce(owner_f[:, :], p3, AX_X, ALU.add).then_inc(s_tab, 1)
            dve.wait_ge(s_tab, 7)
            v.tensor_reduce(start_f[:, 0:BLOCKS], skipped[:, :].rearrange("p (b e) -> p b e", e=n), AX_X,
                            ALU.add).then_inc(s_tab, 1)
            dve.wait_ge(s_tab, 8)
            v.tensor_scalar(owner[:, :], owner_f[:, :], float(EXPERTS - 1), None, ALU.min).then_inc(s_tab, 1)
            dve.wait_ge(s_tab, 10)
            v.tensor_scalar(weights_at[:, :], owner[:, :], float(WCOLS), None, ALU.mult).then_inc(s_tab, 1)
            v.tensor_tensor(start_f[:, BLOCKS:2 * BLOCKS], start_f[:, 0:BLOCKS], const("block_row"),
                            ALU.add).then_inc(s_tab, 1)
            dve.wait_ge(s_tab, 12)
            v.tensor_scalar(start[:, :], start_f[:, BLOCKS:2 * BLOCKS], float(ZERO_LIST), None,
                            ALU.min).then_inc(s_tables, 1)

            def cut(b, k):
                for c in range(HC):
                    a = (k * HC + c) * BLOCK
                    dve.wait_ge(s_gelu, HC * b + c + 1)
                    wait(dve, s_yp, b - 1)
                    v.tensor_scalar(hh[:, a:a + BLOCK], hf[:, a:a + BLOCK], H_SCALE, None,
                                    ALU.mult).then_inc(s_hh, 1)
                    dve.wait_ge(s_hh, HC * b + c + 1)
                    v.scalar_tensor_tensor(out=hl[:, a:a + BLOCK], in0=hf[:, a:a + BLOCK],
                                           scalar=H_SCALE, in1=hh[:, a:a + BLOCK],
                                           op0=ALU.mult, op1=ALU.subtract).then_inc(s_hl, 1)

            def results(b, k, n):
                e = dve.value_load(owner[0:1, ds(b, 1)], min_val=0, max_val=EXPERTS - 1)
                dve.wait_ge(s_yp, b + 1)
                wait(dve, s_part[k], 16 * HALVES * n)
                a = k * HALVES * D
                v.scalar_tensor_tensor(
                    out=y[:, a:a + HALVES * D].rearrange("p (h d) -> p h d", d=D),
                    in0=ps_y[k][:, :].rearrange("p (h d) -> p h d", d=D),
                    scalar=1.0 / (H_SCALE * W_SCALE),
                    in1=b2s[:, ds(e * D, D)].unsqueeze(1).to_broadcast([P, HALVES, D]),
                    op0=ALU.mult, op1=ALU.add).then_inc(s_y, 1)

            dve.wait_ge(s_tables, 2)
            cut(0, 0)
            cut(1, 1)
            results(0, 0, 0)
            cut(2, 0)
            results(1, 1, 0)
            cut(3, 1)
            results(2, 0, 1)
            with dve.Fori(2, BLOCKS // 2) as n:
                cut(2 * n, 0)
                results(2 * n - 1, 1, n - 1)
                cut(2 * n + 1, 1)
                results(2 * n, 0, n)
            results(BLOCKS - 1, 1, BLOCKS // 2 - 1)

            dve.wait_ge(s_ge, 1)
            v.tensor_scalar(gd[:, :], ge[:, :], 1.0, None, ALU.add).then_inc(s_gate, 1)
            dve.wait_ge(s_gate, 1)
            v.reciprocal(g0[:, :], gd[:, :]).then_inc(s_gate, 1)
            dve.wait_ge(s_gate, 2)
            v.tensor_tensor(g1[:, :], g0[:, :], ge[:, :], ALU.mult).then_inc(s_gate, 1)
            dve.wait_ge(s_gate, 3)

            def sums(g, k, n):
                dve.wait_ge(s_pt[k], 32 * (n + 1))
                for r, gate in ((0, g0), (1, g1)):
                    for j in range(GROUP):
                        a = (k * 2 + r) * GROUP * D + j * D
                        xt = X[:, ds((g * GROUP + j) * D, D)]
                        if r == 1:
                            dve.wait_ge(s_sum0, GROUP * g + j + 1)
                        v.scalar_tensor_tensor(
                            out=xt, in0=pt[:, a:a + D], scalar=gate[:, ds(g * GROUP + j, 1)], in1=xt,
                            op0=ALU.mult, op1=ALU.add).then_inc(s_sum0 if r == 0 else s_sum, 1)

            with dve.Fori(0, GROUPS // CR) as n:
                for k in range(CR):
                    sums(n * CR + k, k, n)


def host_constants(tokens, experts, group, block):
    import numpy as np

    p = 128
    tiles = tokens // p
    blocks = 2 * tokens // block + experts
    list_rows = tokens + block

    def rows(a):
        return np.broadcast_to(np.asarray(a, np.float32).reshape(1, -1), (p, np.size(a)))

    parts = [
        np.eye(p, dtype=np.float32),
        rows(np.tile(np.arange(experts), 2 * group)),
        rows(np.tile(np.arange(experts) * list_rows, group)),
        (np.arange(tiles)[None, :] * p + np.arange(p)[:, None]).astype(np.float32),
        (np.arange(p)[:, None] == np.arange(3)[None, :]).astype(np.float32),
        (np.arange(p)[:, None] < 3).astype(np.float32),
        rows(np.arange(blocks) * block),
        rows(np.arange(blocks)),
        rows(np.tile(np.arange(tokens // block) * block, experts)),
        rows(np.zeros(experts)),
        np.full((p, 1), 1e-5 / 256.0 ** 2, np.float32),
    ]
    below = (np.arange(p)[:, None] < np.arange(p)[None, :]).astype(np.float16)
    return (np.ascontiguousarray(np.concatenate(parts, 1)),
            np.ascontiguousarray(np.concatenate([below, np.ones((p, p), np.float16)], 1)))


def kernel(x, adj, L0_gnn_W, L0_gnn_b, L0_ffn_Wg, L0_ffn_bg, L0_ffn_W1, L0_ffn_b1, L0_ffn_W2, L0_ffn_b2):
    import concourse.bacc as bacc
    import numpy as np
    from concourse import mybir
    from concourse.bass_utils import run_bass_kernel_spmd

    x = np.asarray(x)
    w1 = np.asarray(L0_ffn_W1)
    experts, _, h = w1.shape
    consts_f, consts_h = host_constants(x.shape[0] * x.shape[1], experts, 4, 256)
    adj = np.asarray(adj)
    b1 = np.asarray(L0_ffn_b1)
    arrays = {
        "x": x, "adj": adj, "adj_t": adj.T, "gnn_wt": np.asarray(L0_gnn_W).T, "gnn_b": np.asarray(L0_gnn_b),
        "wg": np.asarray(L0_ffn_Wg), "bg": np.asarray(L0_ffn_bg), "w1": w1,
        "b1_t": b1.reshape(experts, h // 128, 128).transpose(2, 0, 1).reshape(128, -1),
        "w2": np.asarray(L0_ffn_W2), "b2": np.asarray(L0_ffn_b2),
        "consts_f": consts_f, "consts_h": consts_h,
    }
    arrays = {k: np.ascontiguousarray(a) for k, a in arrays.items()}
    nc = bacc.Bacc("TRN2", target_bir_lowering=False, num_devices=1)
    args = {k: nc.dram_tensor(f"in_{k}", a.shape, mybir.dt.from_np(a.dtype), kind="ExternalInput").ap()
            for k, a in arrays.items()}
    out = nc.dram_tensor("out_x", x.shape, mybir.dt.float32, kind="ExternalOutput").ap()
    build(nc, **args, out=out)
    result = run_bass_kernel_spmd(nc, [{f"in_{k}": a for k, a in arrays.items()}], core_ids=[0])
    return result.results[0]["out_x"]
```

```python
def build(nc, x, adj, adj_t, gnn_wt, gnn_b, wg, bg, w1, b1_t, w2, b2, consts_f, consts_h, out):
    from contextlib import ExitStack

    import concourse.bass as bass
    from concourse import mybir

    F32, F16, BF16 = mybir.dt.float32, mybir.dt.float16, mybir.dt.bfloat16
    I32, U32 = mybir.dt.int32, mybir.dt.uint32
    ALU = mybir.AluOpType
    ACT = mybir.ActivationFunctionType
    AX_X = mybir.AxisListType.X
    ds = bass.ds

    P = 128
    B, NODES, D = x.shape
    TOKENS = B * NODES
    TILES = TOKENS // P
    EXPERTS, _, H = w1.shape
    GROUP = 4
    GROUPS = TILES // GROUP
    DC, HC = D // P, H // P
    EPS = 1e-5
    X_SCALE = 256.0
    W_SCALE = 1024.0
    H_SCALE = 64.0
    OUT_SCALE = H_SCALE * W_SCALE
    BLOCK = 256
    HALVES = BLOCK // P
    LIST_ROWS = TOKENS + BLOCK
    BLOCKS = 2 * TOKENS // BLOCK + EXPERTS - 1
    ZERO_LIST = EXPERTS * LIST_ROWS
    ROWS = ZERO_LIST + 2 * BLOCK
    TAIL = 16
    ROW32 = D + TAIL
    ROW16 = 2 * ROW32
    RING = 4 * GROUP
    WCOLS = DC * H
    BRING = 4
    ROUNDS, REST = BLOCKS // BRING, BLOCKS % BRING
    WRING = 4
    WSPARE = 8
    LATE = 13
    AHEAD = 7

    col = 0
    cols = {}
    for name, n in (("ident", P), ("iota", 2 * GROUP * EXPERTS), ("list_start", GROUP * EXPERTS),
                    ("token", TILES), ("mask", 3), ("mask3", 1), ("block_row", BLOCKS), ("block", BLOCKS), ("zeros_at", BLOCKS),
                    ("whole", EXPERTS * (TOKENS // BLOCK)), ("zero", EXPERTS), ("spare", 2 * HALVES), ("landed", BLOCKS),
                    ("euler", GROUP), ("eps", 1)):
        cols[name] = (col, n)
        col += n
    NCF = col

    lists = nc.dram_tensor("lists", [ROWS, ROW32], I32).ap()
    lists16 = lists.bitcast(F16)

    with ExitStack() as ctx:
        def sb(name, shape, dt):
            return ctx.enter_context(nc.sbuf_tensor(name, shape, dt))

        leads = []

        def sem(name, lead=0):
            semaphore = ctx.enter_context(nc.semaphore(name))
            if lead:
                leads.append((semaphore, lead))
            return semaphore

        def lead_of(semaphore):
            return sum(lead for other, lead in leads if other is semaphore)

        bank = [ctx.enter_context(nc.psum_tensor(f"bank{i}", [P, 512], F32)) for i in range(8)]
        ps_nb = bank[0:2]
        ps_gnn = bank[2:4]
        ps_score = bank[4]
        ps_place = bank[5]
        ps_h = [bank[0:3], bank[3:6]]
        ps_y = bank[6:8]

        X = sb("X", [P, TILES * D], F32)
        cf = sb("cf", [P, NCF], F32)
        ch = sb("ch", [P, 2 * P], F16)

        def const(name):
            a, n = cols[name]
            return cf[:, a:a + n]

        below, ones = ch[:, 0:P], ch[:, P:2 * P]

        adj_i = sb("adj_i", [P, NODES], I32)
        adj_f = sb("adj_f", [P, NODES], F32)
        adjt_i = sb("adjt_i", [P, P], I32)
        deg = sb("deg", [P, 1], F32)
        nb = sb("nb", [P, 2 * P], F16)
        deg_rows = sb("deg_rows", [P, P], F16)
        gw = sb("gw", [P, 2 * DC * D], F32)
        bias_rows = sb("bias_rows", [P, D], BF16)
        bb = sb("bb", [P, D], F32)
        bpart = sb("bpart", [P, 3 * D], BF16)
        brest = sb("brest", [P, 2 * D], F32)
        bmask = sb("bmask", [P, 2 * D], F32)
        wg_f = sb("wg_f", [P, DC * EXPERTS], F32)
        wg_s = sb("wg_s", [P, DC * EXPERTS], F32)
        wg_h = sb("wg_h", [P, 2 * DC * EXPERTS], F16)
        bgs = sb("bgs", [P, EXPERTS], F32)

        stat1 = sb("stat1", [P, GROUP * 6], F32)
        stat2 = sb("stat2", [P, GROUP * 6], F32)
        mv1 = sb("mv1", [P, GROUP * 2], F32)
        mv2 = sb("mv2", [P, GROUP * 2], F32)
        sd1 = sb("sd1", [P, GROUP], F32)
        sd2 = sb("sd2", [P, GROUP], F32)
        rs1 = sb("rs1", [P, TILES], F32)
        nm1 = sb("nm1", [P, TILES], F32)
        rs2 = sb("rs2", [P, TILES], F32)
        nm2 = sb("nm2", [P, TILES], F32)
        xf1 = sb("xf1", [P, GROUP * D], F32)
        xn1 = sb("xn1", [P, GROUP * 2 * D], F16)
        z = sb("z", [P, 2 * 2 * D], F32)
        xf2 = sb("xf2", [P, 2 * D], F32)
        row = sb("row", [P, RING * ROW32], I32)
        row16 = row[:, :].bitcast(F16)
        row_f = row[:, :].bitcast(F32)
        gT = sb("gT", [P, GROUP * 2 * DC * P], F16)
        score = sb("score", [P, GROUP * EXPERTS], F32)
        best = sb("best", [P, GROUP * 8], F32)
        best_i = sb("best_i", [P, GROUP * 8], U32)
        best_f = sb("best_f", [P, GROUP * 2], F32)
        chose2 = sb("chose2", [P, GROUP * 2 * EXPERTS], F32)
        chose = sb("chose", [P, GROUP * EXPERTS], F16)
        chose_g = sb("chose_g", [P, EXPERTS], F32)
        before = sb("before", [P, EXPERTS], F16)
        counts = sb("counts", [P, GROUPS * EXPERTS], F16)
        place_e = sb("place_e", [P, GROUP * EXPERTS], F32)
        place2 = sb("place2", [P, GROUP * 2 * EXPERTS], F32)
        place_f = sb("place_f", [P, GROUP * 2], F32)
        place = sb("place", [P, RING * 2], I32)
        gap = sb("gap", [P, TILES], F32)
        ge = sb("ge", [P, GROUP], F32)
        gd = sb("gd", [P, GROUP], F32)
        gates = sb("gates", [P, GROUP * 2], F32)
        gate2 = sb("gate2", [P, GROUP * 2 * EXPERTS], F32)

        w_in = sb("w_in", [P, WRING * WCOLS], F32)
        matrix_at = [w_in[:, i * WCOLS:(i + 1) * WCOLS] for i in range(WRING)]
        matrix_at += [X[:, TILES * D - (i + 1) * WCOLS:TILES * D - i * WCOLS] for i in range(WSPARE)]
        w_sc = sb("w_sc", [P, WCOLS], F32)
        cuts = sb("cuts", [P, 4 * EXPERTS * WCOLS], F16)
        w1h, w1l, w2h, w2l = (cuts[:, i * EXPERTS * WCOLS:(i + 1) * EXPERTS * WCOLS] for i in range(4))
        b1s = sb("b1s", [P, EXPERTS * HC], F32)
        b2s = sb("b2s", [P, EXPERTS * D], F32)

        count = sb("count", [P, EXPERTS], F32)
        full = sb("full", [P, EXPERTS * (TOKENS // BLOCK)], F32)
        nblk = sb("nblk", [P, EXPERTS], F32)
        cum = sb("cum", [P, EXPERTS], F32)
        skip = sb("skip", [P, EXPERTS], F32)
        passed = sb("passed", [P, BLOCKS * EXPERTS], F32)
        skipped = sb("skipped", [P, BLOCKS * EXPERTS], F32)
        owner_f = sb("owner_f", [P, BLOCKS], F32)
        start_f = sb("start_f", [P, 2 * BLOCKS], F32)
        owner = sb("owner", [P, BLOCKS], I32)
        weights_at = sb("weights_at", [P, BLOCKS], I32)
        start = sb("start", [P, BLOCKS], I32)
        list_end = sb("list_end", [P, EXPERTS], I32)
        zeros = sb("zeros", [P, 2 * HALVES * ROW32], I32)
        want = sb("want", [P, 2 * EXPERTS], F32)
        lack = sb("lack", [P, GROUPS * EXPERTS], F32)
        lacks = sb("lacks", [P, GROUPS + 1], F32)
        needed = sb("needed", [P, 1], I32)
        past = sb("past", [P, BLOCKS], F32)
        changes = sb("changes", [P, 2 * BLOCKS], F32)
        landed = sb("landed", [P, BLOCKS], I32)

        XCOLS = 2 * DC * BLOCK
        xT = X[:, 0:BRING * XCOLS // 2].bitcast(F16)
        tail = sb("tail", [P, BRING * HALVES * TAIL], I32)
        tail_f = tail[:, :].bitcast(F32)
        HCOLS = 2 * HC * BLOCK
        hf = w_in[:, 0:HCOLS]
        hh = w_in[:, HCOLS:HCOLS + HCOLS // 2].bitcast(F16)
        hl = w_in[:, HCOLS + HCOLS // 2:2 * HCOLS].bitcast(F16)
        y = xf1

        s_const = sem("s_const")
        s_adjz = sem("s_adjz")
        s_b12 = sem("s_b12")
        s_b2 = sem("s_b2")
        s_gap = sem("s_gap")
        s_ge = sem("s_ge", lead=4)
        s_gd = sem("s_gd", lead=4)
        s_g0 = sem("s_g0")
        s_gate = sem("s_gate")
        s_tails = sem("s_tails", lead=4)
        s_spare = sem("s_spare")
        s_adj = sem("s_adj")
        s_setup = sem("s_setup")
        s_nb = sem("s_nb")
        s_degp = sem("s_degp")
        s_deg = sem("s_deg")
        s_bias = sem("s_bias")
        s_wgr = sem("s_wgr")
        s_x = sem("s_x")
        s_bn1 = sem("s_bn1")
        s_mv1 = sem("s_mv1")
        s_sd1 = sem("s_sd1")
        s_sd2 = sem("s_sd2", lead=1)
        s_rs1 = sem("s_rs1")
        s_rs2 = sem("s_rs2", lead=1)
        s_nm1 = sem("s_nm1")
        s_bn2 = sem("s_bn2", lead=4)
        s_mv2 = sem("s_mv2", lead=1)
        s_nm2 = sem("s_nm2", lead=2)
        s_hi1 = sem("s_hi1")
        s_lo1 = sem("s_lo1")
        s_nbp = sem("s_nbp")
        s_z = sem("s_z")
        s_gnn = sem("s_gnn", lead=4)
        s_x1 = sem("s_x1", lead=4)
        s_hi2 = sem("s_hi2", lead=11)
        s_lo2 = sem("s_lo2")
        s_gT = [sem(f"s_gT{j}") for j in range(GROUP)]
        s_sp = sem("s_sp", lead=14)
        s_score = sem("s_score", lead=3)
        s_best = sem("s_best", lead=3)
        s_best_i = sem("s_best_i", lead=3)
        s_best_f = sem("s_best_f", lead=3)
        s_chose2 = sem("s_chose2", lead=3)
        s_chose_g = sem("s_chose_g", lead=4)
        s_chose = sem("s_chose", lead=3)
        s_pp = sem("s_pp", lead=4)
        s_counts = sem("s_counts", lead=4)
        s_ready = sem("s_ready")
        s_place_e = sem("s_place_e", lead=4)
        s_place2 = sem("s_place2", lead=4)
        s_place_f = sem("s_place_f", lead=4)
        s_place = sem("s_place")
        s_scat = [sem(f"s_scat{j}") for j in range(RING // GROUP)]
        s_free = sem("s_free")
        s_w = [sem(f"s_w{k}") for k in range(WRING + WSPARE)]
        s_wsc = sem("s_wsc")
        s_wh = sem("s_wh")
        s_wl = sem("s_wl")
        s_zeros = sem("s_zeros")
        s_cntp = sem("s_cntp")
        s_need = sem("s_need")
        s_tab = sem("s_tab")
        s_tables = sem("s_tables")
        s_pad = sem("s_pad")
        s_listed = sem("s_listed")
        s_xT = [sem(f"s_xT{i}") for i in range(BRING)]
        s_tail = [sem(f"s_tail{i}") for i in range(BRING)]
        s_hp = sem("s_hp")
        s_gelu = sem("s_gelu")
        s_hh = sem("s_hh")
        s_hl = sem("s_hl")
        s_yp = sem("s_yp")
        s_y0 = sem("s_y0")
        s_y = sem("s_y")
        s_part = [sem(f"s_part{k}") for k in range(2)]
        s_out = sem("s_out")
        s_apart = sem("s_apart")

        x_dram = x.rearrange("b k d -> (b k) d").rearrange("(t p) d -> p t d", p=P)
        out_dram = out[0:TOKENS, :].rearrange("(t p) d -> p t d", p=P)
        X3 = X[:, :].rearrange("p (t d) -> p t d", d=D)

        N_CONST = 6

        def in_loop(s):
            return not isinstance(s, int)

        def has(s, g):
            return in_loop(s) or 0 <= g < GROUPS

        def has_tile(s, t):
            return in_loop(s) or 0 <= t < TILES

        def wait(eng, semaphore, value):
            if not isinstance(value, int) or value > 0:
                eng.wait_ge(semaphore, value + lead_of(semaphore))

        def give_leads(eng, *semaphores):
            for semaphore in semaphores:
                eng.sem_inc(semaphore, lead_of(semaphore))

        def apart(eng, s):
            if in_loop(s):
                eng.sem_inc(s_apart, 1)

        def ring(g):
            return (g % (RING // GROUP)) * GROUP

        def zeros_behind(eng, experts):
            for e in experts:
                r = eng.value_load(list_end[0:1, e:e + 1], min_val=0, max_val=ROWS - BLOCK)
                eng.dma_start(lists[ds(r, BLOCK), :].rearrange("(p h) c -> p (h c)", h=HALVES),
                              zeros[:, 0:HALVES * ROW32]).then_inc(s_pad, 16)

        def tails(eng, ops, g, k):
            n = EXPERTS
            first = k * GROUP * ROW32
            span = slice(first, first + GROUP * ROW32)
            ops.tensor_copy(row[:, span].rearrange("p (t c) -> p t c", c=ROW32)[:, :, D],
                                  cf[:, ds(g * GROUP + cols["token"][0], GROUP)])
            eng.wait_ge(s_g0, g + 1)
            ops.tensor_tensor(gates[:, GROUP:2 * GROUP], gates[:, 0:GROUP], ge[:, :],
                                    ALU.mult).then_inc(s_gate, 1)
            wait(eng, s_chose, g + 1)
            eng.wait_ge(s_gate, 2 * g + 1)
            g4 = gate2[:, :].rearrange("p (t r e) -> p t r e", r=2, e=n)
            ops.tensor_tensor(g4, chose2[:, :].rearrange("p (t r e) -> p t r e", r=2, e=n),
                                    gates[:, :].rearrange("p (r t) -> p t r", r=2).unsqueeze(3)
                                    .to_broadcast([P, GROUP, 2, n]), ALU.mult).then_inc(s_gate, 1)
            eng.wait_ge(s_gate, 2 * g + 2)
            ops.tensor_tensor(
                row_f[:, span].rearrange("p (t c) -> p t c", c=ROW32)[:, :, D + 1:D + 1 + n],
                g4[:, :, 0, :], g4[:, :, 1, :], ALU.add).then_inc(s_tails, 1)

        block = ctx.enter_context(nc.Block())

        @block.sync
        def _(sp):
            sp.dma_start(X3[:, 0:GROUP, :], x_dram[:, 0:GROUP, :]).then_inc(s_x, 16)
            w1_dram = w1.rearrange("x (c p) h -> p x c h", p=P)
            w2_dram = w2.rearrange("x (c p) h -> p x c h", p=P)

            def w_load(k):
                e, which = k % EXPERTS, k // EXPERTS
                src = (w1_dram, w2_dram)[which][:, e]
                wait(sp, s_wl, k - len(matrix_at) + 1)
                sp.dma_start(matrix_at[k % len(matrix_at)].rearrange("p (c h) -> p c h", h=src.shape[2]),
                             src).then_inc(s_w[k % len(matrix_at)], 16)

            def x_load(g):
                sp.wait_ge(s_x, 16 * g)
                sp.dma_start(X3[:, g * GROUP:(g + 1) * GROUP, :],
                             x_dram[:, g * GROUP:(g + 1) * GROUP, :]).then_inc(s_x, 16)

            x_load(1)
            for k in range(2 * EXPERTS):
                if k % 3 == 0 and k // 3 + 2 < AHEAD:
                    x_load(k // 3 + 2)
                w_load(k)

            def transposes(g):
                wait(sp, s_x1, GROUP * (g + 1))
                sp.dma_start(out_dram[:, ds(g * GROUP, GROUP), :],
                             X3[:, ds(g * GROUP, GROUP), :]).then_inc(s_out, 16)
                for j in range(GROUP):
                    t = g * GROUP + j
                    sp.wait_ge(s_lo2, t + 1)
                    apart(sp, g)
                    wait(sp, s_sp, t - GROUP + 1)
                    apart(sp, g)
                    sp.dma_start_transpose(
                        gT[:, j * 2 * D:(j + 1) * 2 * D].rearrange("p (c t) -> p c t", t=P),
                        row16[:, ds((ring(g) + j) * ROW16, 2 * D)]).then_inc(s_gT[j], 16)

            def load_and_transpose(g):
                sp.wait_ge(s_x, (g + AHEAD) * 16)
                sp.dma_start(X3[:, ds((g + AHEAD) * GROUP, GROUP), :],
                             x_dram[:, ds((g + AHEAD) * GROUP, GROUP), :]).then_inc(s_x, 16)
                transposes(g)

            sp.wait_ge(s_zeros, 2)
            sp.dma_start(out[TOKENS:TOKENS + 2 * BLOCK, :].rearrange("(p h) d -> p h d", h=2 * HALVES),
                         zeros[:, :].bitcast(F32).rearrange("p (h c) -> p h c", c=ROW32)[:, :, 0:D]
                         ).then_inc(s_spare, 16)
            sp.dma_start(lists[ZERO_LIST:ZERO_LIST + BLOCK, :].rearrange("(p h) c -> p (h c)", h=HALVES),
                         zeros[:, 0:HALVES * ROW32]).then_inc(s_pad, 16)
            sp.dma_start(lists[ZERO_LIST + BLOCK:ROWS, :].rearrange("(p h) c -> p (h c)", h=HALVES),
                         zeros[:, HALVES * ROW32:2 * HALVES * ROW32]).then_inc(s_pad, 16)
            load_and_transpose(0)
            load_and_transpose(1)
            sp.wait_ge(s_wl, WRING + WSPARE)
            with sp.Fori(2, GROUPS - AHEAD) as g:
                load_and_transpose(g)
            with sp.Fori(GROUPS - AHEAD, GROUPS) as g:
                transposes(g)

            sp.wait_ge(s_zeros, 2)
            sp.wait_ge(s_tables, 1)
            zeros_behind(sp, range(0, EXPERTS // 2))
            sp.wait_ge(s_pad, 16 * (EXPERTS + 2))
            sp.wait_ge(s_tables, 2)

            sp.wait_ge(s_out, 16 * GROUPS)

            def load_rows(n, i):
                b = BRING * n + i
                r = sp.value_load(start[0:1, ds(b, 1)], min_val=0, max_val=ROWS - BLOCK)
                wait(sp, s_hp, HC * (b - BRING + 1))
                sp.dma_start_transpose(
                    xT[:, i * XCOLS:(i + 1) * XCOLS].rearrange("p (c t) -> p c t", t=BLOCK),
                    lists16[ds(r, BLOCK), 0:2 * D]).then_inc(s_xT[i], 16)

            def load_tail(n, i):
                b = BRING * n + i
                r = sp.value_load(start[0:1, ds(b, 1)], min_val=0, max_val=ROWS - BLOCK)
                if in_loop(n) or n > 0:
                    sp.wait_ge(s_part[i % 2], 16 * HALVES * (2 * n - 1 + i // 2))
                sp.dma_start(tail[:, i * HALVES * TAIL:(i + 1) * HALVES * TAIL]
                             .rearrange("p (h c) -> p h c", c=TAIL),
                             lists[ds(r, BLOCK), D:ROW32].rearrange("(h p) c -> p h c", p=P)
                             ).then_inc(s_tail[i], 16)

            sp.wait_ge(s_ready, 1)
            groups = sp.value_load(needed[0:1, 0:1], min_val=1, max_val=GROUPS)
            sp.wait_ge(s_free, groups)
            sp.sem_inc(s_apart, 1)
            load_rows(0, 0)
            load_rows(0, 1)
            for i in range(BRING):
                if i < 2:
                    load_rows(0, i + 2)
                load_tail(0, i)
            sp.wait_ge(s_listed, 1)
            load_rows(1, 0)
            load_rows(1, 1)
            with sp.Fori(1, ROUNDS) as n:
                for i in range(BRING):
                    load_rows(*((n, i + 2) if i < 2 else (n + 1, i - 2)))
                    load_tail(n, i)
            for i in range(REST):
                if i + 2 < REST:
                    load_rows(ROUNDS, i + 2)
                load_tail(ROUNDS, i)

        @block.gpsimd
        def _(pool):
            nc.gpsimd.memset(adjt_i[:, :], 0).then_inc(s_adjz, 1)
            give_leads(pool, s_tails, s_ge)
            pool.wait_ge(s_adjz, 1)
            pool.dma_start(adjt_i[0:NODES, 0:NODES], adj_t).then_inc(s_adj, 16)
            pool.dma_start(adjt_i[NODES:P, NODES:P], adj_t).then_inc(s_adj, 16)
            pool.dma_start(adj_i[0:NODES, :], adj).then_inc(s_adj, 16)
            pool.dma_start(adj_i[NODES:P, :], adj).then_inc(s_adj, 16)
            pool.dma_start(b1s[:, :], b1_t).then_inc(s_b12, 16)
            pool.dma_start(b2s[:, :], b2.rearrange("x e -> (x e)").partition_broadcast(P)).then_inc(s_b12, 16)
            nc.gpsimd.memset(zeros[:, :], 0).then_inc(s_zeros, 1)
            row3 = row[:, :].rearrange("p (t c) -> p t c", c=ROW32)
            nc.gpsimd.memset(row3[:, :, D + 1 + EXPERTS:ROW32], 0)

            pool.wait_ge(s_const, 16 * N_CONST)
            pool.wait_ge(s_zeros, 1)
            nc.gpsimd.tensor_copy(zeros[:, :].rearrange("p (h c) -> p h c", c=ROW32)[:, :, D],
                                  const("spare")).then_inc(s_zeros, 1)
            m = const("mask")
            nc.gpsimd.tensor_copy(bpart[:, 0:D], bb[:, :]).then_inc(s_bias, 1)
            pool.wait_ge(s_bias, 1)
            nc.gpsimd.tensor_tensor(brest[:, 0:D], bb[:, :], bpart[:, 0:D], ALU.subtract).then_inc(s_bias, 1)
            pool.wait_ge(s_bias, 2)
            nc.gpsimd.tensor_copy(bpart[:, D:2 * D], brest[:, 0:D]).then_inc(s_bias, 1)
            pool.wait_ge(s_bias, 3)
            nc.gpsimd.tensor_tensor(brest[:, D:2 * D], brest[:, 0:D], bpart[:, D:2 * D],
                                    ALU.subtract).then_inc(s_bias, 1)
            pool.wait_ge(s_bias, 4)
            nc.gpsimd.tensor_copy(bpart[:, 2 * D:3 * D], brest[:, D:2 * D]).then_inc(s_bias, 1)
            pool.wait_ge(s_bias, 5)
            nc.gpsimd.tensor_scalar(bmask[:, 0:D], bpart[:, 0:D], m[:, 0:1], 1.0, ALU.mult, ALU.mult)
            nc.gpsimd.tensor_scalar(bmask[:, D:2 * D], bpart[:, D:2 * D], m[:, 1:2], 1.0,
                                    ALU.mult, ALU.mult).then_inc(s_bias, 1)
            pool.wait_ge(s_bias, 6)
            nc.gpsimd.tensor_tensor(bmask[:, 0:D], bmask[:, 0:D], bmask[:, D:2 * D], ALU.add).then_inc(s_bias, 1)
            pool.wait_ge(s_bias, 7)
            nc.gpsimd.tensor_scalar(bmask[:, D:2 * D], bpart[:, 2 * D:3 * D], m[:, 2:3], 1.0,
                                    ALU.mult, ALU.mult).then_inc(s_bias, 1)
            pool.wait_ge(s_bias, 8)
            nc.gpsimd.tensor_tensor(bias_rows[:, :], bmask[:, 0:D], bmask[:, D:2 * D], ALU.add).then_inc(s_bias, 1)

            for k in range(2 * EXPERTS):
                e, which = k % EXPERTS, k // EXPERTS
                matrix = matrix_at[k % len(matrix_at)]
                hi = (w1h, w2h)[which][:, e * WCOLS:(e + 1) * WCOLS]
                lo = (w1l, w2l)[which][:, e * WCOLS:(e + 1) * WCOLS]
                pool.wait_ge(s_w[k % len(matrix_at)], 16 * (k // len(matrix_at) + 1))
                wait(pool, s_wl, k)
                nc.gpsimd.tensor_scalar(w_sc[:, :], matrix, W_SCALE, 1.0,
                                        ALU.mult, ALU.mult).then_inc(s_wsc, 1)
                pool.wait_ge(s_wsc, k + 1)
                pool.wait_ge(s_wh, k + 1)
                nc.gpsimd.tensor_tensor(lo, w_sc[:, :], hi, ALU.subtract).then_inc(s_wl, 1)

            def exponentials(g):
                wait(pool, s_g0, g)
                if not in_loop(g) and g > LATE:
                    wait(pool, s_tails, g)
                pool.wait_ge(s_gap, g + 1)
                nc.gpsimd.tensor_tensor(ge[:, :], const("euler"), gap[:, ds(g * GROUP, GROUP)],
                                        ALU.pow).then_inc(s_ge, 1)

            def scatters(g, k, half):
                if half == 0:
                    wait(pool, s_tails, g + 1)
                    apart(pool, g)
                    pool.wait_ge(s_place, g + 1)
                    apart(pool, g)
                for j in range(half * GROUP // 2, (half + 1) * GROUP // 2):
                    slot = k * GROUP + j
                    for r in range(2):
                        pool.indirect_dma_start(
                            out=lists,
                            out_offset=bass.IndirectOffsetOnAxis(
                                ap=place[:, 2 * slot + r:2 * slot + r + 1], axis=0),
                            in_=row[:, slot * ROW32:(slot + 1) * ROW32], in_offset=None,
                        ).then_inc(s_scat[k], 16)

            NR = RING // GROUP
            PER = 16 * 2 * GROUP

            def scattered(n, k):
                pool.wait_ge(s_scat[k], PER * (n + 1))
                pool.sem_inc(s_free, 1)

            def turn(g, k, before_this, last=False):
                scatters(g, k, 0)
                if before_this is not None:
                    scattered(before_this, (k - 1) % NR)
                if not last:
                    exponentials(g + 1)
                scatters(g, k, 1)
                if not last and (in_loop(g) or g + 1 < LATE):
                    tails(pool, nc.gpsimd, g + 1, (k + 1) % NR)

            exponentials(0)
            tails(pool, nc.gpsimd, 0, 0)
            for k in range(NR):
                turn(k, k, 0 if k else None)
            with pool.Fori(1, GROUPS // NR - 1) as n:
                for k in range(NR):
                    turn(n * NR + k, k, n if k else n - 1)
            n = GROUPS // NR - 1
            for k in range(NR):
                turn(n * NR + k, k, None if k else n - 1, last=k == NR - 1)
            for k in range(NR):
                pool.wait_ge(s_scat[k], PER * (GROUPS // NR))
            pool.sem_inc(s_free, NR)
            pool.sem_inc(s_listed, 1)

            pool.wait_ge(s_spare, 16)
            pool.wait_ge(s_out, 16 * GROUPS)
            pool.wait_ge(s_tables, 3)

            def add_results(n, i):
                b, k = BRING * n + i, i % 2
                if in_loop(n) or n > 0:
                    before = pool.value_load(landed[0:1, ds(b, 1)], min_val=1, max_val=16 * HALVES * BLOCKS)
                else:
                    before = 16 * HALVES * ((b + 1) // 2)
                pool.wait_ge(s_tail[i], 16 * (n + 1))
                wait(pool, s_part[1 - k], before)
                if in_loop(before):
                    pool.sem_inc(s_apart, 1)
                pool.wait_ge(s_y, HALVES * (b + 1))
                apart(pool, n)
                for h in range(HALVES):
                    at = (i * HALVES + h) * TAIL
                    pool.indirect_dma_start(
                        out=out,
                        out_offset=bass.IndirectOffsetOnAxis(ap=tail[:, at:at + 1], axis=0),
                        in_=y[:, (k * HALVES + h) * D:(k * HALVES + h + 1) * D], in_offset=None,
                        compute_op=ALU.add, bounds_check=TOKENS + 2 * BLOCK - 1,
                    ).then_inc(s_part[k], 16)

            for i in range(BRING):
                add_results(0, i)
            with pool.Fori(1, ROUNDS) as n:
                for i in range(BRING):
                    add_results(n, i)
            for i in range(REST):
                add_results(ROUNDS, i)
            for k in range(2):
                pool.wait_ge(s_part[k], 16 * HALVES * ((BLOCKS + 1 - k) // 2))

        @block.scalar
        def _(act):
            act.dma_start(cf[:, :], consts_f).then_inc(s_const, 16)
            act.dma_start(ch[:, :], consts_h).then_inc(s_const, 16)
            act.dma_start(gw[:, :].rearrange("p (c o) -> p c o", o=D),
                          gnn_wt.rearrange("(c p) o -> p c o", p=P)).then_inc(s_const, 16)
            act.dma_start(bb[:, :], gnn_b.partition_broadcast(P)).then_inc(s_const, 16)
            act.dma_start(wg_f[:, :].rearrange("p (c e) -> p c e", e=EXPERTS),
                          wg.rearrange("(c p) e -> p c e", p=P)).then_inc(s_const, 16)
            act.dma_start(bgs[:, :], bg.partition_broadcast(P)).then_inc(s_const, 16)

            def step(s, j):
                tau = GROUP * s + j
                if has_tile(s, tau):
                    k = j
                    src = X[:, ds(tau * D, D)]
                    wait(act, s_nm1, s + 1)
                    wait(act, s_lo1, tau - 3)
                    wait(act, s_nbp, tau - 3)
                    nc.scalar.activation(xf1[:, k * D:(k + 1) * D], src, ACT.Identity,
                                         bias=nm1[:, ds(tau, 1)], scale=rs1[:, ds(tau, 1)])
                    nc.scalar.activation(xn1[:, k * 2 * D:k * 2 * D + D], src, ACT.Identity,
                                         bias=nm1[:, ds(tau, 1)], scale=rs1[:, ds(tau, 1)]).then_inc(s_hi1, 1)
                if has_tile(s, tau - 3):
                    k = (j + 1) % 2
                    act.wait_ge(s_nbp, tau - 2)
                    wait(act, s_gnn, tau - 4)
                    nc.scalar.activation(z[:, k * 2 * D:(k + 1) * 2 * D], ps_nb[k][:, :], ACT.Copy,
                                         scale=1.0 / X_SCALE).then_inc(s_z, 1)
                if has_tile(s, tau - 11):
                    t = tau - 11
                    g, jj = (s - 2, 0) if j == 3 else (s - 3, j + 1)
                    k = (j + 1) % 2
                    src = X[:, ds(t * D, D)]
                    wait(act, s_nm2, g + 1)
                    wait(act, s_lo2, t - 1)
                    wait(act, s_free, g - RING // GROUP + 1)
                    nc.scalar.activation(xf2[:, k * D:(k + 1) * D], src, ACT.Identity,
                                         bias=nm2[:, ds(t, 1)], scale=rs2[:, ds(t, 1)])
                    nc.scalar.activation(row16[:, ds((ring(g) + jj) * ROW16, D)], src, ACT.Identity,
                                         bias=nm2[:, ds(t, 1)], scale=rs2[:, ds(t, 1)]).then_inc(s_hi2, 1)
                for when, g, mv, sd, mv_ready, sd_ready in ((0, s + 1, mv1, sd1, s_mv1, s_sd1),
                                                            (1, s - 2, mv2, sd2, s_mv2, s_sd2)):
                    if j == when and has(s, g):
                        wait(act, mv_ready, g + 1)
                        nc.scalar.activation(sd[:, :], mv[:, 1:2 * GROUP:2], ACT.Sqrt,
                                             bias=const("eps"), scale=1.0 / X_SCALE ** 2).then_inc(sd_ready, 1)

            give_leads(act, s_hi2, s_sd2)
            act.wait_ge(s_const, 16 * N_CONST)
            for s in range(-1, 7):
                for j in range(GROUP):
                    step(s, j)
            with act.Fori(7, GROUPS - 1) as s:
                for j in range(GROUP):
                    step(s, j)
            for s in range(GROUPS - 1, GROUPS + 3):
                for j in range(GROUP):
                    step(s, j)

            experts = [act.alloc_register(f"expert{k}") for k in range(2)]

            def gelus(b, k):
                act.reg_load(experts[k], owner[0:1, ds(b, 1)])
                e = act.snap(experts[k], donate=False, min_val=0, max_val=EXPERTS - 1)
                for c in range(HC):
                    act.wait_ge(s_hp, HC * b + c + 1)
                    wait(act, s_hl, HC * (b - 2) + c + 1)
                    a = (k * HC + c) * BLOCK
                    nc.scalar.activation(hf[:, a:a + BLOCK], ps_h[k][c][:, 0:BLOCK], ACT.Gelu,
                                         bias=b1s[:, ds(e * HC + c, 1)],
                                         scale=1.0 / (X_SCALE * W_SCALE)).then_inc(s_gelu, 1)

            def weigh(n, i):
                b, k = BRING * n + i, i % 2
                e = act.snap(experts[k], donate=False, min_val=0, max_val=EXPERTS - 1)
                act.wait_ge(s_tail[i], 16 * (n + 1))
                wait(act, s_part[k], 16 * HALVES * (2 * n + i // 2))
                act.wait_ge(s_yp, b + 1)
                for h in range(HALVES):
                    nc.scalar.activation(
                        y[:, (k * HALVES + h) * D:(k * HALVES + h + 1) * D], ps_y[k][:, h * D:(h + 1) * D],
                        ACT.Identity, bias=const("zero")[:, 0:1],
                        scale=tail_f[:, ds(e + ((i * HALVES + h) * TAIL + 1), 1)]).then_inc(s_y0, 1)

            act.wait_ge(s_zeros, 2)
            act.wait_ge(s_tables, 1)
            zeros_behind(act, range(EXPERTS // 2, EXPERTS))
            act.wait_ge(s_tables, 2)
            act.wait_ge(s_b12, 32)
            gelus(0, 0)
            for i in range(1, BRING):
                gelus(i, i % 2)
                weigh(0, i - 1)
            with act.Fori(1, ROUNDS) as n:
                for i in range(BRING):
                    gelus(BRING * n + i, i % 2)
                    weigh(*((n, i - 1) if i else (n - 1, BRING - 1)))
            for i in range(REST):
                gelus(BRING * ROUNDS + i, i % 2)
                weigh(*((ROUNDS, i - 1) if i else (ROUNDS - 1, BRING - 1)))
            weigh(ROUNDS, REST - 1)

        @block.tensor
        def _(pe):
            mm = nc.tensor.matmul
            give_leads(pe, s_gnn, s_sp, s_pp)
            pe.wait_ge(s_const, 16 * N_CONST)
            pe.wait_ge(s_nb, 1)
            mm(ps_place[:, 0:P], ones, nb[:, 0:P], start=True, stop=True).then_inc(s_degp, 1)
            pe.wait_ge(s_deg, 1)
            pe.wait_ge(s_nb, 2)
            pe.wait_ge(s_bias, 9)
            pe.wait_ge(s_wgr, 1)

            def step(s, j):
                tau = GROUP * s + j
                if has_tile(s, tau - 2):
                    k, slot = j % 2, (j + 2) % 4
                    pe.wait_ge(s_lo1, tau - 1)
                    wait(pe, s_z, tau - 3)
                    for c in range(DC):
                        for part in range(2):
                            a = slot * 2 * D + part * D + c * P
                            last = mm(ps_nb[k][:, c * 2 * P:(c + 1) * 2 * P], xn1[:, a:a + P], nb[:, :],
                                      start=part == 0, stop=part == 1)
                    last.then_inc(s_nbp, 1)
                if has_tile(s, tau - 4):
                    k = j % 2
                    o = ps_gnn[k][:, 0:D]
                    pe.wait_ge(s_z, tau - 3)
                    wait(pe, s_x1, tau - 5)
                    mm(o, deg_rows[:, :], bias_rows[:, :], start=True, stop=False)
                    for c in range(DC):
                        a = k * 2 * D + c * 2 * P
                        mm(o, z[:, a:a + P], gw[:, (DC + c) * D:(DC + c + 1) * D], start=False, stop=False)
                        last = mm(o, z[:, a + P:a + 2 * P], gw[:, c * D:(c + 1) * D],
                                  start=False, stop=c == DC - 1)
                    last.then_inc(s_gnn, 1)
                if j == 0 and has(s, s - 5):
                    g = s - 5
                    wait(pe, s_chose, g + 1)
                    n = EXPERTS
                    mm(ps_place[:, 0:GROUP * n], below, chose[:, :], start=True, stop=False)
                    for i in range(GROUP):
                        mm(ps_place[:, i * n:(i + 1) * n], ones, before[:, :], start=False, stop=False)
                        for q in range(i):
                            last = mm(ps_place[:, i * n:(i + 1) * n], ones, chose[:, q * n:(q + 1) * n],
                                      start=False, stop=(i, q) == (GROUP - 1, GROUP - 2))
                    last.then_inc(s_pp, 1)
                if has_tile(s, tau - 14):
                    g, jj = (s - 4, j + 2) if j < 2 else (s - 3, j - 2)
                    pe.wait_ge(s_gT[jj], 16 * (g + 1))
                    wait(pe, s_score, g)
                    o = ps_score[:, jj * EXPERTS:(jj + 1) * EXPERTS]
                    for c in range(DC):
                        hi = gT[:, jj * 2 * D + c * P:jj * 2 * D + (c + 1) * P]
                        lo = gT[:, jj * 2 * D + D + c * P:jj * 2 * D + D + (c + 1) * P]
                        wh = wg_h[:, c * EXPERTS:(c + 1) * EXPERTS]
                        wl = wg_h[:, (DC + c) * EXPERTS:(DC + c + 1) * EXPERTS]
                        mm(o, hi, wl, start=c == 0, stop=False)
                        mm(o, lo, wh, start=False, stop=False)
                        last = mm(o, hi, wh, start=False, stop=c == DC - 1)
                    last.then_inc(s_sp, 1)

            for s in range(0, 5):
                for j in range(GROUP):
                    step(s, j)
            with pe.Fori(5, GROUPS) as s:
                for j in range(GROUP):
                    step(s, j)
            for s in range(GROUPS, GROUPS + 6):
                for j in range(GROUP):
                    step(s, j)
            pe.wait_ge(s_place, GROUPS)
            mm(ps_place[:, 0:GROUPS * EXPERTS], ones, counts[:, :], start=True, stop=True).then_inc(s_cntp, 1)

            w_at = [pe.alloc_register(f"w_at{k}") for k in range(2)]

            def owner_weights(b, k):
                pe.reg_load(w_at[k], weights_at[0:1, ds(b, 1)])

            def base(k):
                return pe.snap(w_at[k], donate=False, min_val=0, max_val=(EXPERTS - 1) * WCOLS)

            def hidden(n, i):
                b, k = BRING * n + i, i % 2
                owner_weights(b, k)
                w0 = base(k)
                pe.wait_ge(s_xT[i], 16 * (n + 1))
                wait(pe, s_gelu, HC * (b - 1))
                for h in range(HC):
                    o = ps_h[k][h][:, 0:BLOCK]
                    for c in range(DC):
                        a = i * XCOLS + c * BLOCK
                        hi, lo = xT[:, a:a + BLOCK], xT[:, a + DC * BLOCK:a + (DC + 1) * BLOCK]
                        w = ds(w0 + (c * H + h * P), P)
                        mm(o, w1l[:, w], hi, start=c == 0, stop=False)
                        mm(o, w1h[:, w], lo, start=False, stop=False)
                        last = mm(o, w1h[:, w], hi, start=False, stop=c == DC - 1)
                    last.then_inc(s_hp, 1)

            def output(b, k):
                w0 = base(k)
                wait(pe, s_y0, HALVES * (b - 1))
                for h in range(HC):
                    pe.wait_ge(s_hl, HC * b + h + 1)
                    w = ds(w0 + h * D, D)
                    for left, right in ((hl, w2h), (hh, w2h), (hh, w2l)):
                        for m in range(HALVES):
                            a = (k * HC + h) * BLOCK + m * P
                            last = mm(ps_y[k][:, m * D:(m + 1) * D], left[:, a:a + P], right[:, w],
                                      start=(h, m) == (0, 0) and left is hl,
                                      stop=(h, m) == (HC - 1, 1) and right is w2l,
                                      skip_group_check=True)
                last.then_inc(s_yp, 1)

            pe.wait_ge(s_tables, 2)
            pe.wait_ge(s_wl, 2 * EXPERTS)
            hidden(0, 0)
            for i in range(1, BRING):
                hidden(0, i)
                output(i - 1, (i - 1) % 2)
            with pe.Fori(1, ROUNDS) as n:
                for i in range(BRING):
                    hidden(n, i)
                    output(BRING * n + i - 1, (i - 1) % 2)
            for i in range(REST):
                hidden(ROUNDS, i)
                output(BRING * ROUNDS + i - 1, (i - 1) % 2)
            output(BLOCKS - 1, (REST - 1) % 2)

        @block.vector
        def _(dve):
            v = nc.vector
            give_leads(dve, s_x1, s_bn2, s_mv2, s_nm2, s_rs2, s_chose, s_gd, s_score, s_best, s_best_i,
                       s_best_f, s_chose2, s_chose_g, s_counts, s_place_e, s_place2, s_place_f)

            def set_up():
                dve.wait_ge(s_const, 16 * N_CONST)
                dve.wait_ge(s_adj, 64)
                v.tensor_copy(nb[:, 0:P], adjt_i[:, :]).then_inc(s_nb, 1)
                v.tensor_copy(adj_f[:, :], adj_i[:, :]).then_inc(s_setup, 1)
                v.tensor_scalar(wg_s[:, :], wg_f[:, :], W_SCALE, None, ALU.mult).then_inc(s_setup, 1)
                v.memset(before[:, :], 0.0)
                dve.wait_ge(s_setup, 1)
                v.tensor_reduce(deg[:, :], adj_f[:, :], AX_X, ALU.add).then_inc(s_setup, 1)
                NW = DC * EXPERTS
                dve.wait_ge(s_setup, 2)
                v.tensor_copy(wg_h[:, 0:NW], wg_s[:, :]).then_inc(s_setup, 1)
                dve.wait_ge(s_setup, 3)
                v.tensor_scalar(nb[:, P:2 * P], const("ident"), deg[:, 0:1], None, ALU.mult).then_inc(s_nb, 1)
                dve.wait_ge(s_setup, 4)
                v.tensor_tensor(wg_h[:, NW:2 * NW], wg_s[:, :], wg_h[:, 0:NW], ALU.subtract).then_inc(s_wgr, 1)
                dve.wait_ge(s_degp, 1)
                v.tensor_scalar(deg_rows[:, :], ps_place[:, 0:P], const("mask3"), None, ALU.mult).then_inc(s_deg, 1)

            def cut_weights(k):
                e, which = k % EXPERTS, k // EXPERTS
                dve.wait_ge(s_w[k % len(matrix_at)], 16 * (k // len(matrix_at) + 1))
                v.tensor_scalar((w1h, w2h)[which][:, e * WCOLS:(e + 1) * WCOLS], matrix_at[k % len(matrix_at)],
                                W_SCALE, None, ALU.mult).then_inc(s_wh, 1)

            def inverse(g, sd, rs, sd_ready, rs_ready, now):
                dve.wait_ge(sd_ready, now)
                v.reciprocal(rs[:, ds(g * GROUP, GROUP)], sd[:, :]).then_inc(rs_ready, 1)

            def shifts(g, mv, rs, nm, rs_ready, nm_ready, now):
                dve.wait_ge(rs_ready, now)
                v.scalar_tensor_tensor(
                    out=nm[:, ds(g * GROUP, GROUP)], in0=mv[:, 0:2 * GROUP:2], scalar=-1.0,
                    in1=rs[:, ds(g * GROUP, GROUP)], op0=ALU.mult, op1=ALU.mult).then_inc(nm_ready, 1)

            def aggregate(g, stat, mv, bn_ready, bn_now, mv_ready, nm_ready, now):
                if in_loop(now) or now > 0:
                    dve.wait_ge(nm_ready, now)
                dve.wait_ge(bn_ready, bn_now)
                apart(dve, g)
                for i in range(GROUP):
                    last = v.bn_aggr(mv[:, 2 * i:2 * i + 2], stat[:, 6 * i:6 * i + 6])
                last.then_inc(mv_ready, 1)

            def step(s, j, ahead):
                tau = GROUP * s + j
                now = dve.snap(tau) if in_loop(s) else tau
                slot = s
                choosing = j == 2 and has(s, s - 4)
                placing = j == 1 and has(s, s - 5)
                early = in_loop(s) or 0 <= s - 5 < LATE
                if j == 2 and has(s, s - 5) and not early:
                    gate_divisors(slot)
                    best_gates(slot)
                    tails(dve, v, s - 5, (s - 5) % (RING // GROUP))
                if placing:
                    expert_places(slot)
                if choosing:
                    g = s - 4
                    dve.wait_ge(s_sp, now)
                    v.scalar_tensor_tensor(
                        out=score[:, :].rearrange("p (t e) -> p t e", e=EXPERTS),
                        in0=ps_score[:, 0:GROUP * EXPERTS].rearrange("p (t e) -> p t e", e=EXPERTS),
                        scalar=1.0 / (X_SCALE * W_SCALE),
                        in1=bgs[:, :].unsqueeze(1).to_broadcast([P, GROUP, EXPERTS]),
                        op0=ALU.mult, op1=ALU.add).then_inc(s_score, 1)
                if has_tile(s, tau - 1):
                    k = (j + 3) % 4
                    dve.wait_ge(s_hi1, now)
                    v.tensor_tensor(xn1[:, k * 2 * D + D:(k + 1) * 2 * D], xf1[:, k * D:(k + 1) * D],
                                    xn1[:, k * 2 * D:k * 2 * D + D], ALU.subtract).then_inc(s_lo1, 1)
                if j == 0 and early:
                    gate_divisors(slot)
                if placing:
                    note_counts(s - 5, slot)
                if choosing:
                    best_scores(s - 4, slot)
                if j == 3 and has(s, s - 4):
                    group_counts(s - 4, slot)
                if has_tile(s, tau - 5):
                    k = (j + 1) % 2
                    xt = X[:, ds((tau - 5) * D, D)]
                    dve.wait_ge(s_gnn, now)
                    v.tensor_tensor(xt, ps_gnn[k][:, 0:D], xt, ALU.add).then_inc(s_x1, 1)
                if j == 0 and early:
                    best_gates(slot)
                if placing:
                    chosen_places(slot)
                if choosing:
                    best_indices(s - 4, slot)
                if j == 1 and has(s, s + 1):
                    inverse(s + 1, sd1, rs1, s_sd1, s_rs1, ahead)
                if j == 2 and has(s, s - 2):
                    inverse(s - 2, sd2, rs2, s_sd2, s_rs2, slot)
                if has_tile(s, tau + 8):
                    g, jj = s + 2, j
                    if jj == 0 or not in_loop(s):
                        dve.wait_ge(s_x, 16 * (g + 1))
                    if jj == 0:
                        wait(dve, s_mv1, ahead)
                        apart(dve, s)
                    v.bn_stats(stat1[:, jj * 6:jj * 6 + 6], X[:, ds((tau + 8) * D, D)]).then_inc(s_bn1, 1)
                if placing:
                    add_counts(slot)
                    sum_places(slot)
                if choosing:
                    indices_as_floats(s - 4, slot)
                if has_tile(s, tau - 5):
                    jj = (j + 3) % 4
                    if jj == 0:
                        dve.wait_ge(s_mv2, slot)
                    dve.wait_ge(s_x1, now)
                    apart(dve, s)
                    v.bn_stats(stat2[:, jj * 6:jj * 6 + 6], X[:, ds((tau - 5) * D, D)]).then_inc(s_bn2, 1)
                if placing:
                    write_places(s - 5, slot)
                if choosing:
                    one_hot(s - 4, slot)
                if j == 1 and has(s, s + 1):
                    shifts(s + 1, mv1, rs1, nm1, s_rs1, s_nm1, ahead)
                if j == 2 and has(s, s - 2):
                    shifts(s - 2, mv2, rs2, nm2, s_rs2, s_nm2, slot)
                if has_tile(s, tau - 12):
                    g, k = s - 3, j % 2
                    a = (ring(g) + j) * ROW16
                    dve.wait_ge(s_hi2, now)
                    v.tensor_tensor(row16[:, ds(a + D, D)], xf2[:, k * D:(k + 1) * D],
                                    row16[:, ds(a, D)], ALU.subtract).then_inc(s_lo2, 1)
                if choosing:
                    either(s - 4, slot)
                if j == 3 and has(s, s + 2):
                    aggregate(s + 2, stat1, mv1, s_bn1, GROUP * (s + 3), s_mv1, s_nm1, ahead)
                if j == 0 and has(s, s - 2):
                    aggregate(s - 2, stat2, mv2, s_bn2, now, s_mv2, s_nm2, slot)

            n = EXPERTS

            def best_scores(g, slot):
                dve.wait_ge(s_score, slot)
                apart(dve, g)
                for i in range(GROUP):
                    last = v.max(best[:, 8 * i:8 * i + 8], score[:, n * i:n * (i + 1)])
                last.then_inc(s_best, 1)

            def best_indices(g, slot):
                dve.wait_ge(s_best, slot)
                apart(dve, g)
                for i in range(GROUP):
                    last = v.max_index(best_i[:, 8 * i:8 * i + 8], best[:, 8 * i:8 * i + 8],
                                       score[:, n * i:n * (i + 1)])
                last.then_inc(s_best_i, 1)

            def indices_as_floats(g, slot):
                b3 = best[:, :].rearrange("p (t k) -> p t k", k=8)
                v.tensor_tensor(gap[:, ds(g * GROUP, GROUP)], b3[:, :, 1], b3[:, :, 0],
                                ALU.subtract).then_inc(s_gap, 1)
                dve.wait_ge(s_best_i, slot)
                v.tensor_copy(best_f[:, :].rearrange("p (t r) -> p t r", r=2),
                              best_i[:, :].rearrange("p (t k) -> p t k", k=8)[:, :, 0:2]).then_inc(s_best_f, 1)

            def one_hot(g, slot):
                dve.wait_ge(s_best_f, slot)
                dve.wait_ge(s_tails, slot)
                v.tensor_tensor(chose2[:, :].rearrange("p (q e) -> p q e", e=n),
                                const("iota").rearrange("p (q e) -> p q e", e=n),
                                best_f[:, :].unsqueeze(2).to_broadcast([P, 2 * GROUP, n]),
                                ALU.is_equal).then_inc(s_chose2, 1)

            def either(g, slot):
                dve.wait_ge(s_chose2, slot)
                c4 = chose2[:, :].rearrange("p (t r e) -> p t r e", r=2, e=n)
                v.tensor_tensor(chose[:, :].rearrange("p (t e) -> p t e", e=n),
                                c4[:, :, 0, :], c4[:, :, 1, :], ALU.add).then_inc(s_chose, 1)

            def group_counts(g, slot):
                dve.wait_ge(s_chose, slot)
                v.tensor_reduce(chose_g[:, :], chose[:, :].rearrange("p (t e) -> p e t", e=n),
                                AX_X, ALU.add).then_inc(s_chose_g, 1)

            def gate_divisors(slot):
                dve.wait_ge(s_ge, slot)
                v.tensor_scalar(gd[:, :], ge[:, :], 1.0, OUT_SCALE, ALU.add, ALU.mult).then_inc(s_gd, 1)

            def best_gates(slot):
                dve.wait_ge(s_gd, slot)
                v.reciprocal(gates[:, 0:GROUP], gd[:, :]).then_inc(s_g0, 1)

            def expert_places(slot):
                dve.wait_ge(s_pp, slot)
                v.tensor_tensor(place_e[:, :], ps_place[:, 0:GROUP * n], const("list_start"),
                                ALU.add).then_inc(s_place_e, 1)

            def note_counts(g, slot):
                dve.wait_ge(s_chose_g, slot)
                v.tensor_tensor(counts[:, ds(g * n, n)], before[:, :], chose_g[:, :],
                                ALU.add).then_inc(s_counts, 1)

            def add_counts(slot):
                dve.wait_ge(s_counts, slot)
                v.tensor_tensor(before[:, :], before[:, :], chose_g[:, :], ALU.add)

            def chosen_places(slot):
                dve.wait_ge(s_place_e, slot)
                v.tensor_tensor(place2[:, :].rearrange("p (t r e) -> p t r e", r=2, e=n),
                                chose2[:, :].rearrange("p (t r e) -> p t r e", r=2, e=n),
                                place_e[:, :].rearrange("p (t e) -> p t e", e=n).unsqueeze(2)
                                .to_broadcast([P, GROUP, 2, n]), ALU.mult).then_inc(s_place2, 1)

            def sum_places(slot):
                dve.wait_ge(s_place2, slot)
                v.tensor_reduce(place_f[:, :], place2[:, :].rearrange("p (q e) -> p q e", e=n), AX_X,
                                ALU.add).then_inc(s_place_f, 1)

            def write_places(g, slot):
                dve.wait_ge(s_place_f, slot)
                v.tensor_copy(place[:, ds(2 * ring(g), 2 * GROUP)], place_f[:, :]).then_inc(s_place, 1)

            def tables():
                dve.wait_ge(s_b12, 32)
                v.tensor_scalar(b2s[:, :], b2s[:, :], OUT_SCALE, None, ALU.mult).then_inc(s_b2, 1)
                dve.wait_ge(s_b2, 1)

                most = TOKENS // BLOCK
                dve.wait_ge(s_cntp, 1)
                v.tensor_copy(count[:, :], ps_place[:, (GROUPS - 1) * n:GROUPS * n]).then_inc(s_tab, 1)
                dve.wait_ge(s_tab, 1)
                v.tensor_tensor(list_end[:, :], count[:, :], const("list_start")[:, 0:n], ALU.add).then_inc(s_tables, 1)
                v.tensor_tensor(full[:, :].rearrange("p (e k) -> p e k", k=most),
                                count[:, :].unsqueeze(2).to_broadcast([P, n, most]),
                                const("whole").rearrange("p (e k) -> p e k", k=most), ALU.is_gt).then_inc(s_tab, 1)
                dve.wait_ge(s_tab, 2)
                v.tensor_reduce(nblk[:, :], full[:, :].rearrange("p (e k) -> p e k", k=most), AX_X,
                                ALU.add).then_inc(s_tab, 1)
                dve.wait_ge(s_tab, 3)
                v.tensor_tensor_scan(cum[:, :], nblk[:, :], const("zero"), 0.0, ALU.add, ALU.add).then_inc(s_tab, 1)
                v.tensor_scalar(skip[:, :], nblk[:, :], -float(BLOCK), float(LIST_ROWS), ALU.mult,
                                ALU.add).then_inc(s_tab, 1)
                dve.wait_ge(s_tab, 5)
                p3 = passed[:, :].rearrange("p (b e) -> p b e", e=n)
                v.tensor_tensor(p3, cum[:, :].unsqueeze(1).to_broadcast([P, BLOCKS, n]),
                                const("block").unsqueeze(2).to_broadcast([P, BLOCKS, n]),
                                ALU.is_le).then_inc(s_tab, 1)
                dve.wait_ge(s_tab, 6)
                v.tensor_tensor(skipped[:, :].rearrange("p (b e) -> p b e", e=n), p3,
                                skip[:, :].unsqueeze(1).to_broadcast([P, BLOCKS, n]), ALU.mult).then_inc(s_tab, 1)
                v.tensor_reduce(owner_f[:, :], p3, AX_X, ALU.add).then_inc(s_tab, 1)
                dve.wait_ge(s_tab, 7)
                v.tensor_reduce(start_f[:, 0:BLOCKS], skipped[:, :].rearrange("p (b e) -> p b e", e=n), AX_X,
                                ALU.add).then_inc(s_tab, 1)
                dve.wait_ge(s_tab, 8)
                v.tensor_scalar(owner[:, :], owner_f[:, :], float(EXPERTS - 1), None, ALU.min).then_inc(s_tab, 1)
                dve.wait_ge(s_tab, 10)
                v.tensor_scalar(weights_at[:, :], owner[:, :], float(WCOLS), None, ALU.mult).then_inc(s_tab, 1)
                v.tensor_scalar(past[:, :], owner_f[:, :], float(EXPERTS), 2.0 * BLOCK, ALU.is_ge, ALU.mult)
                v.tensor_tensor(start_f[:, BLOCKS:2 * BLOCKS], start_f[:, 0:BLOCKS], const("block_row"),
                                ALU.add).then_inc(s_tab, 1)
                dve.wait_ge(s_tab, 12)
                v.tensor_tensor(start_f[:, 0:BLOCKS], start_f[:, BLOCKS:2 * BLOCKS], past[:, :],
                                ALU.add).then_inc(s_tab, 1)
                dve.wait_ge(s_tab, 13)
                v.tensor_tensor(start[:, :], start_f[:, 0:BLOCKS], const("zeros_at"),
                                ALU.min).then_inc(s_tables, 1)
                v.tensor_tensor(want[:, 0:n], nblk[:, :], cum[:, :], ALU.subtract).then_inc(s_need, 1)
                dve.wait_ge(s_need, 1)
                v.tensor_scalar(want[:, n:2 * n], want[:, 0:n], float(BRING), 0.0, ALU.add,
                                ALU.max).then_inc(s_need, 1)
                dve.wait_ge(s_need, 2)
                v.scalar_tensor_tensor(out=want[:, 0:n], in0=want[:, n:2 * n], scalar=float(BLOCK),
                                       in1=count[:, :], op0=ALU.mult, op1=ALU.min).then_inc(s_need, 1)
                dve.wait_ge(s_need, 3)
                v.tensor_tensor(lack[:, :].rearrange("p (g e) -> p g e", e=n),
                                ps_place[:, 0:GROUPS * n].rearrange("p (g e) -> p g e", e=n),
                                want[:, 0:n].unsqueeze(1).to_broadcast([P, GROUPS, n]), ALU.is_lt).then_inc(s_need, 1)
                dve.wait_ge(s_need, 4)
                v.tensor_reduce(lacks[:, 0:GROUPS], lack[:, :].rearrange("p (g e) -> p g e", e=n), AX_X,
                                ALU.max).then_inc(s_need, 1)
                dve.wait_ge(s_need, 5)
                v.tensor_reduce(lacks[:, GROUPS:GROUPS + 1], lacks[:, 0:GROUPS], AX_X, ALU.add).then_inc(s_need, 1)
                dve.wait_ge(s_need, 6)
                v.tensor_scalar(needed[:, :], lacks[:, GROUPS:GROUPS + 1], 1.0, None, ALU.add).then_inc(s_ready, 1)
                c0, c1 = (changes[:, i * BLOCKS:(i + 1) * BLOCKS] for i in range(2))
                v.memset(c0[:, 0:1], 1.0)
                v.tensor_tensor(c0[:, 1:BLOCKS], owner_f[:, 1:BLOCKS], owner_f[:, 0:BLOCKS - 1],
                                ALU.subtract).then_inc(s_tab, 1)
                dve.wait_ge(s_tab, 14)
                v.tensor_scalar(c1, c0, 1.0, 16.0 * HALVES, ALU.min, ALU.mult).then_inc(s_tab, 1)
                dve.wait_ge(s_tab, 15)
                v.tensor_tensor(landed[:, :], c1, const("landed"), ALU.add).then_inc(s_tables, 1)

            k = 0
            for s in range(-2, 5):
                if s == -1:
                    set_up()
                for j in range(GROUP):
                    step(s, j, s + 2)
                    if s >= 0 and k < 2 * EXPERTS:
                        cut_weights(k)
                        k += 1
            with dve.Fori(5, GROUPS - 2) as s:
                ahead = dve.snap(s + 2)
                for j in range(GROUP):
                    step(s, j, ahead)
            for s in range(GROUPS - 2, GROUPS + 5):
                for j in range(GROUP):
                    if (s, j) == (GROUPS + 4, 2):
                        tables()
                    step(s, j, s + 2)

            experts = {}

            def cut(b, k):
                if not (isinstance(b, int) and b == 0):
                    experts[1 - k] = dve.value_load(owner[0:1, ds(b - 1, 1)], min_val=0, max_val=EXPERTS - 1)
                for c in range(HC):
                    a = (k * HC + c) * BLOCK
                    dve.wait_ge(s_gelu, HC * b + c + 1)
                    wait(dve, s_yp, b - 1)
                    v.tensor_scalar(hh[:, a:a + BLOCK], hf[:, a:a + BLOCK], H_SCALE, None,
                                    ALU.mult).then_inc(s_hh, 1)
                    dve.wait_ge(s_hh, HC * b + c + 1)
                    v.scalar_tensor_tensor(out=hl[:, a:a + BLOCK], in0=hf[:, a:a + BLOCK],
                                           scalar=H_SCALE, in1=hh[:, a:a + BLOCK],
                                           op0=ALU.mult, op1=ALU.subtract).then_inc(s_hl, 1)

            def results(n, i):
                b, k = BRING * n + i, i % 2
                e = experts[k]
                for h in range(HALVES):
                    yh = y[:, (k * HALVES + h) * D:(k * HALVES + h + 1) * D]
                    dve.wait_ge(s_y0, HALVES * b + h + 1)
                    v.scalar_tensor_tensor(
                        out=yh, in0=b2s[:, ds(e * D, D)], scalar=tail_f[:, ds(e + ((i * HALVES + h) * TAIL + 1), 1)],
                        in1=yh, op0=ALU.mult, op1=ALU.add).then_inc(s_y, 1)

            dve.wait_ge(s_tables, 2)
            cut(0, 0)
            for i in range(1, BRING):
                cut(i, i % 2)
                results(0, i - 1)
            with dve.Fori(1, ROUNDS) as n:
                for i in range(BRING):
                    cut(BRING * n + i, i % 2)
                    results(*((n, i - 1) if i else (n - 1, BRING - 1)))
            for i in range(REST):
                cut(BRING * ROUNDS + i, i % 2)
                results(*((ROUNDS, i - 1) if i else (ROUNDS - 1, BRING - 1)))
            experts[(REST - 1) % 2] = dve.value_load(owner[0:1, BLOCKS - 1:BLOCKS], min_val=0, max_val=EXPERTS - 1)
            results(ROUNDS, REST - 1)


def host_constants(tokens, experts, group, block):
    import numpy as np

    p = 128
    tiles = tokens // p
    blocks = 2 * tokens // block + experts - 1
    list_rows = tokens + block

    def rows(a):
        return np.broadcast_to(np.asarray(a, np.float32).reshape(1, -1), (p, np.size(a)))

    parts = [
        np.eye(p, dtype=np.float32),
        rows(np.tile(np.arange(experts), 2 * group)),
        rows(np.tile(np.arange(experts) * list_rows, group)),
        (np.arange(tiles)[None, :] * p + np.arange(p)[:, None]).astype(np.float32),
        (np.arange(p)[:, None] == np.arange(3)[None, :]).astype(np.float32),
        (np.arange(p)[:, None] < 3).astype(np.float32),
        rows(np.arange(blocks) * block),
        rows(np.arange(blocks)),
        rows(experts * list_rows + np.arange(blocks) % 2 * block),
        rows(np.tile(np.arange(tokens // block) * block, experts)),
        rows(np.zeros(experts)),
        (tokens + np.arange(p)[:, None] * (block // p) + np.arange(block // p)[None, :]).astype(np.float32),
        (tokens + block + np.arange(p)[:, None] * (block // p) + np.arange(block // p)[None, :]).astype(np.float32),
        rows(16 * (block // p) * ((np.arange(blocks) - 1) // 2)),
        rows(np.e * np.ones(group)),
        np.full((p, 1), 1e-5 / 256.0 ** 2, np.float32),
    ]
    below = (np.arange(p)[:, None] < np.arange(p)[None, :]).astype(np.float16)
    return (np.ascontiguousarray(np.concatenate(parts, 1)),
            np.ascontiguousarray(np.concatenate([below, np.ones((p, p), np.float16)], 1)))


def kernel(x, adj, L0_gnn_W, L0_gnn_b, L0_ffn_Wg, L0_ffn_bg, L0_ffn_W1, L0_ffn_b1, L0_ffn_W2, L0_ffn_b2):
    import concourse.bacc as bacc
    import numpy as np
    from concourse import mybir
    from concourse.bass_utils import run_bass_kernel_spmd

    x = np.asarray(x)
    w1 = np.asarray(L0_ffn_W1)
    experts, _, h = w1.shape
    consts_f, consts_h = host_constants(x.shape[0] * x.shape[1], experts, 4, 256)
    adj = np.asarray(adj)
    b1 = np.asarray(L0_ffn_b1)
    arrays = {
        "x": x, "adj": adj, "adj_t": adj.T, "gnn_wt": np.asarray(L0_gnn_W).T, "gnn_b": np.asarray(L0_gnn_b),
        "wg": np.asarray(L0_ffn_Wg), "bg": np.asarray(L0_ffn_bg), "w1": w1,
        "b1_t": b1.reshape(experts, h // 128, 128).transpose(2, 0, 1).reshape(128, -1),
        "w2": np.asarray(L0_ffn_W2), "b2": np.asarray(L0_ffn_b2),
        "consts_f": consts_f, "consts_h": consts_h,
    }
    arrays = {k: np.ascontiguousarray(a) for k, a in arrays.items()}
    nc = bacc.Bacc("TRN2", target_bir_lowering=False, num_devices=1)
    args = {k: nc.dram_tensor(f"in_{k}", a.shape, mybir.dt.from_np(a.dtype), kind="ExternalInput").ap()
            for k, a in arrays.items()}
    tokens = x.shape[0] * x.shape[1]
    out = nc.dram_tensor("out_x", [tokens + 2 * 256, x.shape[2]], mybir.dt.float32, kind="ExternalOutput").ap()
    build(nc, **args, out=out)
    result = run_bass_kernel_spmd(nc, [{f"in_{k}": a for k, a in arrays.items()}], core_ids=[0])
    return result.results[0]["out_x"][:tokens].reshape(x.shape)
```
